# Optimizing a Trainium2 kernel written in Bass

```python
import numpy as np
import jax
import jax.numpy as jnp

def _softmax(x, axis=-1):
    return jax.nn.softmax(x, axis=axis)

def _gelu(x):
    return jax.nn.gelu(x, approximate=True)

def _silu(x):
    return jax.nn.silu(x)

def _sigmoid(x):
    return jax.nn.sigmoid(x)

def _layernorm(x, axis=-1, eps=1e-05):
    m = jnp.mean(x, axis=axis, keepdims=True)
    v = jnp.var(x, axis=axis, keepdims=True)
    return (x - m) / jnp.sqrt(v + eps)

def _scatter_add(tgt, idx, src, axis=0):
    return tgt.at[idx].add(src)

def _segment_sum(src, seg, n):
    return jax.ops.segment_sum(src, seg, n)
kernel_name = 'mk_rec_standalone_d1_rec_r8_6dc839'

def setup_inputs(seed: int=0):
    np.random.seed(seed)
    _w = jnp.asarray

    def _rec_inputs():
        import jax
        import jax.numpy as jnp
        _rk = jax.random.key(seed)
        r_Xi = jnp.stack([jax.random.randint(jax.random.fold_in(jax.random.fold_in(_rk, 1), 0), (2048,), 2, 6250, jnp.int32), jax.random.randint(jax.random.fold_in(jax.random.fold_in(_rk, 1), 1), (2048,), 0, 49999, jnp.int32), jax.random.randint(jax.random.fold_in(jax.random.fold_in(_rk, 1), 2), (2048,), 0, 49995, jnp.int32), jax.random.randint(jax.random.fold_in(jax.random.fold_in(_rk, 1), 3), (2048,), 1, 49991, jnp.int32), jax.random.randint(jax.random.fold_in(jax.random.fold_in(_rk, 1), 4), (2048,), 0, 6249, jnp.int32), jax.random.randint(jax.random.fold_in(jax.random.fold_in(_rk, 1), 5), (2048,), 5, 6250, jnp.int32), jax.random.randint(jax.random.fold_in(jax.random.fold_in(_rk, 1), 6), (2048,), 4, 6250, jnp.int32), jax.random.randint(jax.random.fold_in(jax.random.fold_in(_rk, 1), 7), (2048,), 1, 6250, jnp.int32), jax.random.randint(jax.random.fold_in(jax.random.fold_in(_rk, 1), 8), (2048,), 0, 49991, jnp.int32), jax.random.randint(jax.random.fold_in(jax.random.fold_in(_rk, 1), 9), (2048,), 0, 49994, jnp.int32), jax.random.randint(jax.random.fold_in(jax.random.fold_in(_rk, 1), 10), (2048,), 1, 6250, jnp.int32), jax.random.randint(jax.random.fold_in(jax.random.fold_in(_rk, 1), 11), (2048,), 4, 49998, jnp.int32), jax.random.randint(jax.random.fold_in(jax.random.fold_in(_rk, 1), 12), (2048,), 2, 49994, jnp.int32), jax.random.randint(jax.random.fold_in(jax.random.fold_in(_rk, 1), 13), (2048,), 4, 49999, jnp.int32), jax.random.randint(jax.random.fold_in(jax.random.fold_in(_rk, 1), 14), (2048,), 7, 49996, jnp.int32), jax.random.randint(jax.random.fold_in(jax.random.fold_in(_rk, 1), 15), (2048,), 1, 49995, jnp.int32), jax.random.randint(jax.random.fold_in(jax.random.fold_in(_rk, 1), 16), (2048,), 0, 49997, jnp.int32), jax.random.randint(jax.random.fold_in(jax.random.fold_in(_rk, 1), 17), (2048,), 3, 49998, jnp.int32), jax.random.randint(jax.random.fold_in(jax.random.fold_in(_rk, 1), 18), (2048,), 1, 49998, jnp.int32), jax.random.randint(jax.random.fold_in(jax.random.fold_in(_rk, 1), 19), (2048,), 5, 6249, jnp.int32), jax.random.randint(jax.random.fold_in(jax.random.fold_in(_rk, 1), 20), (2048,), 7, 6250, jnp.int32), jax.random.randint(jax.random.fold_in(jax.random.fold_in(_rk, 1), 21), (2048,), 7, 49997, jnp.int32), jax.random.randint(jax.random.fold_in(jax.random.fold_in(_rk, 1), 22), (2048,), 1, 49993, jnp.int32), jax.random.randint(jax.random.fold_in(jax.random.fold_in(_rk, 1), 23), (2048,), 2, 49999, jnp.int32), jax.random.randint(jax.random.fold_in(jax.random.fold_in(_rk, 1), 24), (2048,), 0, 49998, jnp.int32), jax.random.randint(jax.random.fold_in(jax.random.fold_in(_rk, 1), 25), (2048,), 4, 6249, jnp.int32), jax.random.randint(jax.random.fold_in(jax.random.fold_in(_rk, 1), 26), (2048,), 0, 6250, jnp.int32), jax.random.randint(jax.random.fold_in(jax.random.fold_in(_rk, 1), 27), (2048,), 3, 6250, jnp.int32), jax.random.randint(jax.random.fold_in(jax.random.fold_in(_rk, 1), 28), (2048,), 0, 6250, jnp.int32), jax.random.randint(jax.random.fold_in(jax.random.fold_in(_rk, 1), 29), (2048,), 8, 49999, jnp.int32), jax.random.randint(jax.random.fold_in(jax.random.fold_in(_rk, 1), 30), (2048,), 0, 6250, jnp.int32), jax.random.randint(jax.random.fold_in(jax.random.fold_in(_rk, 1), 31), (2048,), 0, 6250, jnp.int32)], axis=1)
        return r_Xi
    r_Xi = _rec_inputs()

    def _L0_rec_setup():
        import jax, jax.numpy as jnp
        import numpy as np
        B, F, V, E, H, L = (2048, 32, 6250, 64, 4, 3)
        HD = E // H
        D1, D2 = (1024, 512)

        def layer_norm(x, gamma, beta, eps=1e-05):
            mu = jnp.mean(x, axis=-1, keepdims=True)
            var = jnp.mean((x - mu) ** 2, axis=-1, keepdims=True)
            return (x - mu) * jax.lax.rsqrt(var + eps) * gamma + beta

        def mha(x, Wqkv, bqkv, Wo, bo):
            b, f, e = x.shape
            qkv = x @ Wqkv.T + bqkv
            q, k, v = jnp.split(qkv, 3, axis=-1)
            split = lambda t: t.reshape(b, f, H, HD).transpose(0, 2, 1, 3)
            q, k, v = (split(q), split(k), split(v))
            scores = jnp.einsum('bhqd,bhkd->bhqk', q, k) / np.sqrt(HD)
            attn = jax.nn.softmax(scores, axis=-1)
            o = jnp.einsum('bhqk,bhkd->bhqd', attn, v)
            o = o.transpose(0, 2, 1, 3).reshape(b, f, e)
            return o @ Wo.T + bo
        key = jax.random.key(seed)
        ks = jax.random.split(key, 20)
        s = 0.05
        inp = {'Xi': jax.random.randint(ks[0], (B, F), 0, V), 'Xv': jax.random.uniform(ks[1], (B, F, 1), dtype=jnp.float32), 'tables': jax.random.normal(ks[2], (F, V, E), dtype=jnp.float32) * 0.01, 'Wqkv': jax.random.normal(ks[3], (L, 3 * E, E), dtype=jnp.float32) * s, 'bqkv': jnp.zeros((L, 3 * E), jnp.float32), 'Wo': jax.random.normal(ks[4], (L, E, E), dtype=jnp.float32) * s, 'bo': jnp.zeros((L, E), jnp.float32), 'Wr': jax.random.normal(ks[5], (E, E), dtype=jnp.float32) * s, 'br': jnp.zeros((E,), jnp.float32), 'gamma': jnp.ones((E,), jnp.float32), 'beta': jnp.zeros((E,), jnp.float32), 'Wf': jax.random.normal(ks[6], (F * E, 1), dtype=jnp.float32) * s, 'bf': jnp.zeros((1,), jnp.float32), 'W1': jax.random.normal(ks[7], (F * E, D1), dtype=jnp.float32) * s, 'b1': jnp.zeros((D1,), jnp.float32), 'W2': jax.random.normal(ks[8], (D1, D2), dtype=jnp.float32) * s, 'b2': jnp.zeros((D2,), jnp.float32), 'Wd': jax.random.normal(ks[9], (D2, 1), dtype=jnp.float32) * s, 'bd': jnp.zeros((1,), jnp.float32)}
        return inp
    _L0_rec_all = _L0_rec_setup()
    _L0_rec_in = {k: v for k, v in _L0_rec_all.items() if k in ('Xv', 'tables', 'Wqkv', 'bqkv', 'Wo', 'bo', 'Wr', 'br', 'gamma', 'beta', 'Wf', 'bf', 'W1', 'b1', 'W2', 'b2', 'Wd', 'bd')}
    del _L0_rec_all
    return {'r_Xi': r_Xi, 'L0_rec_Xv': _L0_rec_in['Xv'], 'L0_rec_tables': _L0_rec_in['tables'], 'L0_rec_Wqkv': _L0_rec_in['Wqkv'], 'L0_rec_bqkv': _L0_rec_in['bqkv'], 'L0_rec_Wo': _L0_rec_in['Wo'], 'L0_rec_bo': _L0_rec_in['bo'], 'L0_rec_Wr': _L0_rec_in['Wr'], 'L0_rec_br': _L0_rec_in['br'], 'L0_rec_gamma': _L0_rec_in['gamma'], 'L0_rec_beta': _L0_rec_in['beta'], 'L0_rec_Wf': _L0_rec_in['Wf'], 'L0_rec_bf': _L0_rec_in['bf'], 'L0_rec_W1': _L0_rec_in['W1'], 'L0_rec_b1': _L0_rec_in['b1'], 'L0_rec_W2': _L0_rec_in['W2'], 'L0_rec_b2': _L0_rec_in['b2'], 'L0_rec_Wd': _L0_rec_in['Wd'], 'L0_rec_bd': _L0_rec_in['bd']}

def reference(r_Xi, L0_rec_Xv, L0_rec_tables, L0_rec_Wqkv, L0_rec_bqkv, L0_rec_Wo, L0_rec_bo, L0_rec_Wr, L0_rec_br, L0_rec_gamma, L0_rec_beta, L0_rec_Wf, L0_rec_bf, L0_rec_W1, L0_rec_b1, L0_rec_W2, L0_rec_b2, L0_rec_Wd, L0_rec_bd):
    import jax
    import jax.numpy as jnp

    def _L0_rec_ref(Xi, Xv, tables, Wqkv, bqkv, Wo, bo, Wr, br, gamma, beta, Wf, bf, W1, b1, W2, b2, Wd, bd):
        import jax, jax.numpy as jnp
        import numpy as np
        B, F, V, E, H, L = (2048, 32, 6250, 64, 4, 3)
        HD = E // H
        D1, D2 = (1024, 512)

        def layer_norm(x, gamma, beta, eps=1e-05):
            mu = jnp.mean(x, axis=-1, keepdims=True)
            var = jnp.mean((x - mu) ** 2, axis=-1, keepdims=True)
            return (x - mu) * jax.lax.rsqrt(var + eps) * gamma + beta

        def mha(x, Wqkv, bqkv, Wo, bo):
            b, f, e = x.shape
            qkv = x @ Wqkv.T + bqkv
            q, k, v = jnp.split(qkv, 3, axis=-1)
            split = lambda t: t.reshape(b, f, H, HD).transpose(0, 2, 1, 3)
            q, k, v = (split(q), split(k), split(v))
            scores = jnp.einsum('bhqd,bhkd->bhqk', q, k) / np.sqrt(HD)
            attn = jax.nn.softmax(scores, axis=-1)
            o = jnp.einsum('bhqk,bhkd->bhqd', attn, v)
            o = o.transpose(0, 2, 1, 3).reshape(b, f, e)
            return o @ Wo.T + bo
        emb = tables[jnp.arange(F), Xi] * Xv
        att = emb
        for l in range(L):
            o = mha(att, Wqkv[l], bqkv[l], Wo[l], bo[l])
            o = o + jax.nn.relu(att @ Wr.T + br)
            o = jax.nn.relu(o)
            att = layer_norm(o, gamma, beta)
        att_logit = att.reshape(B, -1) @ Wf + bf
        h = jax.nn.relu(emb.reshape(B, -1) @ W1 + b1)
        h = jax.nn.relu(h @ W2 + b2)
        dnn_logit = h @ Wd + bd
        return att_logit + dnn_logit
    y = _L0_rec_ref(r_Xi, L0_rec_Xv, L0_rec_tables, L0_rec_Wqkv, L0_rec_bqkv, L0_rec_Wo, L0_rec_bo, L0_rec_Wr, L0_rec_br, L0_rec_gamma, L0_rec_beta, L0_rec_Wf, L0_rec_bf, L0_rec_W1, L0_rec_b1, L0_rec_W2, L0_rec_b2, L0_rec_Wd, L0_rec_bd)
    return y

_drawn_inputs = setup_inputs


def setup_inputs(seed=0):
    import zlib

    import numpy as np

    out = dict(_drawn_inputs(seed))
    spreads = {'L0_rec_bqkv': (0.0, 0.1),
     'L0_rec_bo': (0.0, 0.1),
     'L0_rec_br': (0.0, 0.1),
     'L0_rec_gamma': (1.0, 0.2),
     'L0_rec_beta': (0.0, 0.1),
     'L0_rec_b1': (0.0, 0.1),
     'L0_rec_b2': (0.0, 0.1)}
    factors = {'L0_rec_Xv': 3.568, 'L0_rec_W1': 8.0, 'L0_rec_W2': 3.88}
    for name, (base, spread) in spreads.items():
        noise = np.random.default_rng([zlib.crc32(name.encode()), seed]).standard_normal(out[name].shape)
        drawn = base * np.exp(spread * noise) if base else spread * noise
        out[name] = jnp.asarray(drawn.astype(out[name].dtype))
    for name, factor in factors.items():
        out[name] = (out[name] * factor).astype(out[name].dtype)
    return out
```

```python
from contextlib import ExitStack

import concourse.bass as bass
from concourse import mybir

F32 = mybir.dt.float32
BF16 = mybir.dt.bfloat16
I32 = mybir.dt.int32
ALU = mybir.AluOpType
ACT = mybir.ActivationFunctionType
AX = mybir.AxisListType

B, F, V, E, H, L = 2048, 32, 6250, 64, 4, 3
HD = E // H
D1, D2 = 1024, 512
P = 128
NJ = B // P
NDG = NJ // 2
PAIRS = 16
TOK = PAIRS * F
NT = B // (2 * PAIRS)
PB = P // PAIRS
PQ = PAIRS // 4
SLOTS = NT * L
INFLIGHT = 4
BODY = INFLIGHT * L
LEAD = 5
TURNS = (SLOTS - LEAD) // BODY
KC = F * E // P
KC2 = D1 // P
EPS = 1e-5
SCALE = 1.0 / float(HD) ** 0.5
VC = E + H


def build(nc, Xi, Xv, tables, WqkvT, bqkv, WoT, bo, WrT, br, gamma, beta, Wf, bf,
          W1, b1, W2, b2, Wd, bd, ident_in, out):
    xT_dram = nc.dram_tensor("xT_scratch", (NT, P, TOK), F32, kind="Internal").ap()
    v_dram = nc.dram_tensor("v_scratch", (2, P, TOK), F32, kind="Internal").ap()
    with ExitStack() as ctx:
        def sb(name, shape, dt=F32, to=ctx):
            return to.enter_context(nc.sbuf_tensor(name, shape, dt))

        def sem(name):
            return ctx.enter_context(nc.semaphore(name))

        bank = [ctx.enter_context(nc.psum_tensor(f"bank{i}", [P, 512], F32)) for i in range(8)]
        ident = sb("ident", [P, P])
        dnn = sb("dnn", [P, NJ])
        wd_b = sb("wd_b", [P, D2])
        misc_loaded = sem("misc_loaded")

        phase_one(nc, ctx, sb, sem, bank, ident, dnn, wd_b, misc_loaded, xT_dram,
                  Xi, Xv, tables, W1, b1, W2, b2, Wd, ident_in)
        phase_two(nc, ctx, sb, sem, bank, ident, dnn, xT_dram, v_dram,
                  WqkvT, bqkv, WoT, bo, WrT, br, gamma, beta, Wf, bf, bd, out)


def phase_one(nc, ctx, sb, sem, bank, ident, dnn, wd_b, misc_loaded, xT_dram,
              Xi, Xv, tables, W1, b1, W2, b2, Wd, ident_in):
    with ExitStack() as ph:
        def s1(name, shape, dt=F32):
            return sb(name, shape, dt, ph)

        w1 = s1("w1", [P, KC, D1])
        w2 = s1("w2", [P, KC2, D2])
        b1r = s1("b1r", [1, D1])
        b2r = s1("b2r", [1, D2])
        ones1 = s1("ones1", [1, P])
        xi = s1("xi", [P, NJ * F], I32)
        base = s1("base", [P, NJ * F], I32)
        neg = s1("neg", [P, NJ * F], I32)
        xv = s1("xv", [P, NJ * F])
        idx = [s1(f"idx{u}", [P, 2 * F], I32) for u in range(2)]
        emb = [s1(f"emb{u}", [P, 2, F, E]) for u in range(2)]
        pairs = s1("pairs", [P, F, 2, E])
        xt = s1("xt", [P, P, F])
        et = [s1(f"et{g}", [P, KC, P]) for g in range(2)]
        turn = s1("turn", [1, 1])
        h1 = s1("h1", [P, D1])
        h1t = s1("h1t", [P, KC2, P])
        h2 = s1("h2", [P, D2])
        h2w = s1("h2w", [P, D2])
        logit = s1("logit", [P, 1])

        setup_loaded = sem("setup_loaded")
        w_loaded = sem("w_loaded")
        base_ready = sem("base_ready")
        idx_all = sem("idx_all")
        ones_ready = sem("ones_ready")
        idx_cur = sem("idx_cur")
        gather_turn = sem("gather_turn")
        gathered = [sem(f"gathered{u}") for u in range(2)]
        emb_scaled = sem("emb_scaled")
        emb_read = sem("emb_read")
        xt_banks = sem("xt_banks")
        xt_turned = sem("xt_turned")
        xt_stored = sem("xt_stored")
        pairs_ready = sem("pairs_ready")
        et_turned = sem("et_turned")
        et_copied = sem("et_copied")
        h1_done = sem("h1_done")
        h1_relu = sem("h1_relu")
        h1t_turned = sem("h1t_turned")
        h1t_copied = sem("h1t_copied")
        h2_done = sem("h2_done")
        h2_relu = sem("h2_relu")
        dnn_done = sem("dnn_done")
        dnn_stored = sem("dnn_stored")

        block = ph.enter_context(nc.Block())

        @block.sync
        def _(sp):
            sp.dma_start(xi[:], Xi.rearrange("(p j) f -> p (j f)", j=NJ)).then_inc(setup_loaded, 16)
            sp.dma_start(xv[:], Xv.rearrange("(p j) f o -> p (j f o)", j=NJ)).then_inc(setup_loaded, 16)
            sp.dma_start(ident[:], ident_in).then_inc(setup_loaded, 16)
            sp.dma_start(b1r[:], b1.rearrange("(o n) -> o n", o=1)).then_inc(w_loaded, 16)
            sp.dma_start(b2r[:], b2.rearrange("(o n) -> o n", o=1)).then_inc(w_loaded, 16)
            sp.dma_start(wd_b[:], Wd.rearrange("n o -> (n o)").partition_broadcast(P)).then_inc(w_loaded, 16)
            sp.dma_start(w1[:], W1.rearrange("(c p) n -> p c n", p=P)).then_inc(w_loaded, 16)
            sp.dma_start(w2[:], W2.rearrange("(c p) n -> p c n", p=P)).then_inc(w_loaded, 16)
            with sp.Fori(0, NDG // 2) as k:
                for u in range(2):
                    sp.wait_ge(xt_banks, 2 + 8 * (2 * k + u + 1))
                    sp.dma_start(xT_dram[bass.ds((2 * k + u) * PB, PB)].rearrange("t p c -> p t c"),
                                 xt[:, :, :].rearrange("p (t a) f -> p t (a f)", t=PB)
                                 ).then_inc(xt_stored, 16)
            sp.wait_ge(xt_stored, 16 * NDG)

        @block.gpsimd
        def _(pool):
            pool.iota(base[:], [[0, NJ], [V, F]], base=0, channel_multiplier=0).then_inc(base_ready, 1)
            pool.memset(turn[:], 0.0).then_inc(base_ready, 1)
            pool.wait_ge(base_ready, 2)
            pool.wait_ge(idx_all, 4)
            rows = tables.rearrange("f v e -> (f v) e")
            for u in range(2):
                gather(nc, pool, u, u, idx, xi, idx_cur, emb, rows, gathered, turn, gather_turn)
            with pool.Fori(1, NDG // 2) as k:
                for u in range(2):
                    pool.wait_ge(gathered[u], 32 * F * k)
                    pool.wait_ge(emb_read, 2 * k + u - 1)
                    gather(nc, pool, 2 * k + u, u, idx, xi, idx_cur, emb, rows, gathered, turn, gather_turn)

        @block.vector
        def _(dve):
            dve.memset(ones1[:], 1.0).then_inc(ones_ready, 1)
            dve.wait_ge(setup_loaded, 48)
            dve.wait_ge(base_ready, 2)
            dve.tensor_scalar(neg[:], xi[:], 0.0, float(V), ALU.is_lt, ALU.mult).then_inc(idx_all, 1)
            dve.wait_ge(idx_all, 1)
            dve.tensor_tensor(neg[:], xi[:], neg[:], ALU.add).then_inc(idx_all, 1)
            dve.wait_ge(idx_all, 2)
            dve.tensor_scalar(neg[:], neg[:], float(V - 1), 0.0, ALU.min, ALU.max).then_inc(idx_all, 1)
            dve.wait_ge(idx_all, 3)
            dve.tensor_tensor(xi[:], neg[:], base[:], ALU.add).then_inc(idx_all, 1)
            dve.wait_ge(w_loaded, 80)
            with dve.Fori(0, NDG // 2) as k:
                for u in range(2):
                    d = 2 * k + u
                    dve.wait_ge(gathered[u], 32 * F * (k + 1))
                    xvd = xv[:, bass.ds(d * 2 * F, 2 * F)].rearrange("p (n o) -> p n o", o=1)\
                        .to_broadcast([P, 2 * F, E])
                    dve.wait_ge(xt_turned, 8 * d)
                    dve.tensor_tensor(pairs[:].rearrange("p f g e -> p g f e"), emb[u][:],
                                      xvd.rearrange("p (g f) e -> p g f e", g=2), ALU.mult).then_inc(pairs_ready, 1)
                    dve.wait_ge(pairs_ready, d + 1)
                    flat = emb[u][:, :, :, :].rearrange("p g f e -> p (g f) e")
                    dve.tensor_tensor(flat, flat, xvd, ALU.mult).then_inc(emb_scaled, 1)
                    for g in range(2):
                        j = 2 * d + g
                        for c in range(4):
                            dve.wait_ge(et_turned, 4 * j + c + 1)
                            dve.tensor_copy(et[g][:, 4 * c:4 * c + 4, :],
                                            bank[2 + c % 2][:, :].rearrange("p (a b) -> p a b", a=4)
                                            ).then_inc(et_copied, 1)
                    for g in range(2):
                        j = 2 * d + g
                        for c in range(2):
                            dve.wait_ge(h1t_turned, 2 * j + c + 1)
                            dve.tensor_copy(h1t[:, 4 * c:4 * c + 4, :],
                                            bank[2 + c][:, :].rearrange("p (a b) -> p a b", a=4)
                                            ).then_inc(h1t_copied, 1)
                        dve.wait_ge(h2_relu, j + 1)
                        dve.tensor_tensor_reduce(h2w[:], h2[:], wd_b[:], 1.0, 0.0, ALU.mult, ALU.add,
                                                 logit[:]).then_inc(dnn_done, 1)
                        dve.wait_ge(dnn_done, j + 1)
                        dve.tensor_copy(dnn[:, bass.ds(j, 1)], logit[:]).then_inc(dnn_stored, 1)
                        dve.wait_ge(dnn_stored, j + 1)

        @block.scalar
        def _(act):
            act.wait_ge(ones_ready, 1)
            act.activation(h2[0:1, 0:P], ones1[:], ACT.Copy).then_inc(xt_banks, 2)
            with act.Fori(0, NDG // 2) as k:
                for u in range(2):
                    d = 2 * k + u
                    act.wait_ge(xt_stored, 16 * d)
                    for c in range(8):
                        act.wait_ge(xt_turned, 8 * d + c + 1)
                        act.activation(xt[:, :, 4 * c:4 * c + 4].rearrange("p a f -> p f a"),
                                       bank[c % 2][:, :].rearrange("p (f a) -> p f a", f=4),
                                       ACT.Copy).then_inc(xt_banks, 1)
                    for g in range(2):
                        j = 2 * d + g
                        for n in range(2):
                            act.wait_ge(h1_done, 2 * j + n + 1)
                            if g == 0 and n == 0:
                                act.wait_ge(h1t_turned, 2 * j)
                            act.activation(h1[:, 512 * n:512 * n + 512], bank[4 + n][:, :],
                                           ACT.Relu).then_inc(h1_relu, 1)
                        act.wait_ge(h2_done, j + 1)
                        act.wait_ge(dnn_done, j)
                        act.activation(h2[:], bank[6][:, :], ACT.Relu).then_inc(h2_relu, 1)

        @block.tensor
        def _(pe):
            pe.wait_ge(setup_loaded, 48)
            pe.wait_ge(ones_ready, 1)
            pe.wait_ge(w_loaded, 80)
            with pe.Fori(0, NDG // 2) as k:
                for u in range(2):
                    d = 2 * k + u
                    pe.wait_ge(pairs_ready, d + 1)
                    for c in range(8):
                        pe.wait_ge(xt_banks, 8 * d + c + 1)
                        for i in range(4):
                            last = pe.transpose(bank[c % 2][:, P * i:P * i + P],
                                                pairs[:, 4 * c + i, :, :], ident[:])
                        last.then_inc(xt_turned, 1)
                    for g in range(2):
                        j = 2 * d + g
                        pe.wait_ge(emb_scaled, d + 1)
                        for c in range(4):
                            if c >= 2:
                                pe.wait_ge(et_copied, 4 * j + c - 1)
                            elif g == 1:
                                pe.wait_ge(et_copied, 4 * j + c - 1)
                            else:
                                pe.wait_ge(h1t_copied, 2 * j)
                            for i in range(4):
                                m = 4 * c + i
                                last = pe.transpose(bank[2 + c % 2][:, P * i:P * i + P],
                                                    emb[u][:, g, 2 * m:2 * m + 2, :], ident[:])
                            last.then_inc(et_turned, 1)
                        if g == 1:
                            pe.transpose(bank[7][:, 0:P], ident[:], ident[:]).then_inc(emb_read, 1)
                    for g in range(2):
                        j = 2 * d + g
                        pe.wait_ge(et_copied, 4 * j + 4)
                        if g == 1:
                            pe.wait_ge(h1_relu, 2 * j)
                        else:
                            pe.wait_ge(h1_relu, 2 * j)
                        for n in range(2):
                            cols = slice(512 * n, 512 * n + 512)
                            pe.matmul(bank[4 + n][:, :], ones1[:], b1r[:, cols], start=True, stop=False)
                            for c in range(KC):
                                last = pe.matmul(bank[4 + n][:, :], et[g][:, c, :], w1[:, c, cols],
                                                 start=False, stop=(c == KC - 1))
                            last.then_inc(h1_done, 1)
                        pe.wait_ge(h1_relu, 2 * j + 2)
                        pe.wait_ge(h1t_copied, 2 * j)
                        pe.wait_ge(et_copied, 8 * d + 8)
                        for c in range(2):
                            for i in range(4):
                                m = 4 * c + i
                                last = pe.transpose(bank[2 + c][:, P * i:P * i + P],
                                                    h1[:, P * m:P * m + P], ident[:])
                            last.then_inc(h1t_turned, 1)
                        pe.wait_ge(h2_relu, j)
                        pe.matmul(bank[6][:, :], ones1[:], b2r[:], start=True, stop=False)
                        pe.wait_ge(h1t_copied, 2 * j + 2)
                        for c in range(KC2):
                            last = pe.matmul(bank[6][:, :], h1t[:, c, :], w2[:, c, :],
                                             start=False, stop=(c == KC2 - 1))
                        last.then_inc(h2_done, 1)


def gather(nc, pool, d, u, idx, xi, idx_cur, emb, rows, gathered, turn, gather_turn):
    pool.tensor_copy(idx[u][:], xi[:, bass.ds(d * 2 * F, 2 * F)]).then_inc(idx_cur, 1)
    pool.wait_ge(idx_cur, d + 1)
    pool.tensor_tensor(turn[:], turn[:], turn[:], ALU.mult).then_inc(gather_turn, 1)
    for g in range(2):
        for f in range(F):
            pool.indirect_dma_start(emb[u][:, g, f, :], None, rows,
                                    bass.IndirectOffsetOnAxis(idx[u][:, g * F + f:g * F + f + 1], 0)
                                    ).then_inc(gathered[u], 16)


def phase_two(nc, ctx, sb, sem, bank, ident, dnn, xT_dram, v_dram,
              WqkvT, bqkv, WoT, bo, WrT, br, gamma, beta, Wf, bf, bd, out):
    w = sb("w", [P, L, 5 * P])
    QC, KCOL, VR, OC = 0, P, 2 * P, 4 * P
    bq = sb("bq", [P, L])
    bk = sb("bk", [P, L])
    bqm = sb("bqm", [P, L, 2])
    gmask = sb("gmask", [P, 2])
    qmask = sb("qmask", [P, 2])
    hmask = sb("hmask", [P, H])
    gam = sb("gam", [P, 1])
    bet = sb("bet", [P, 1])
    wf = sb("wf", [P, F])
    bfd = sb("bfd", [P, 2])
    bias_f = sb("bias_f", [3, L, 2, 512])
    bias_t = sb("bias_t", [3, L, 2, 512])
    part = [sb(f"bias_part{i}", [3, L, 2, 512], BF16) for i in range(3)]
    bias3 = sb("bias3", [3, L, 2, 512], BF16)
    ones3 = sb("ones3", [3, P], BF16)
    mhalf = sb("mhalf", [P, 2 * PQ])
    turn = sb("turn2", [1, 1])

    x = [sb(f"x{i}", [P, TOK]) for i in range(INFLIGHT)]
    xf = [sb(f"xf{i}", [P, PAIRS, F]) for i in range(2)]
    xw = sb("xw", [P, PAIRS, F])
    z = sb("z", [P, NT * PAIRS])
    kt = sb("kt", [P, TOK])
    qg = [sb(f"qg{i}", [P, PAIRS, 2, F]) for i in range(2)]
    kh = [sb(f"kh{i}", [P, PAIRS, H, F]) for i in range(2)]
    v = [sb(f"v{i}", [P, E, 2, PQ]) for i in range(2)]
    vbd = [sb(f"vbd{i}", [P, 4, VC, 2 * PQ]) for i in range(2)]
    r = [sb(f"r{i}", [P, PQ, P]) for i in range(4)]
    smax = sb("smax", [P, 2, PAIRS])
    s = sb("s", [P, 2, PAIRS, F])
    pr = sb("pr", [P, 2, PAIRS * F])
    pt = [sb(f"pt{i}", [P, 2, PAIRS * F]) for i in range(2)]
    rden = sb("rden", [P, 2 * PQ, H])
    on = sb("on", [P, 2 * PQ, E])
    ot = sb("ot", [P, TOK])
    y = sb("y", [P, 2 * PQ, E])
    ysum = sb("ysum", [P, 2 * PQ])
    cen = sb("cen", [P, 2 * PQ, E])
    sq = sb("sq", [P, 2 * PQ, E])
    sqs = sb("sqs", [P, 2 * PQ])
    var = sb("var", [P, 2 * PQ])
    rstd = sb("rstd", [P, 2 * PQ])
    xn = sb("xn", [P, 2 * PQ, E])
    res = sb("res", [P, NJ])

    names = """consts_zeroed consts_loaded wf_loaded ones_set bias_step consts_ready vbd_zeroed vbd_ready
        k_done q_done vr_done s_done0 s_done1 pv_done ot_done o_done xt_done
        k_ready q_ready kh_turn kh_ready r_ready v_ready ot_ready x_ready
        max_step s_sub0 s_sub1 exp_done0 exp_done1 pt_turned0 pt_turned1 pt_ready0 pt_ready1
        rden_ready on_ready y_sum_ready y_ready ysum_ready cen_ready sq_ready sqs_ready var_ready
        rstd_ready xn_ready xw_ready z_ready att_done res_step out_stored""".split()
    S = {n: sem(n) for n in names}
    x_loaded = [sem(f"x_loaded{i}") for i in range(INFLIGHT)]
    v_stored = [sem(f"v_stored{i}") for i in range(2)]
    v_loaded = [sem(f"v_loaded{i}") for i in range(2)]

    def after(b, k, per=1):
        return (b + 1) * per + BODY * per * k

    def after2(b, k, per):
        return (b // 2 + 1) * per + BODY // 2 * per * k

    def over_slots(eng, stages):
        for m in range(LEAD):
            stages(m, 0)
        with eng.Fori(0, TURNS) as k:
            for m in range(LEAD, LEAD + BODY):
                stages(m, k)
        for m in range(LEAD + BODY * TURNS, SLOTS + 4):
            stages(m, 0)

    def live(n):
        return 0 <= n < SLOTS

    block = ctx.enter_context(nc.Block())

    @block.sync
    def _(sp):
        sp.wait_ge(S["consts_zeroed"], 1)
        for l in range(L):
            for g in range(2):
                rows = slice(E * g, E * g + E)
                for col, part_w in ((QC, WqkvT[l, :, 0:E]), (KCOL, WqkvT[l, :, E:2 * E]),
                                    (VR, WqkvT[l, :, 2 * E:3 * E]), (VR + P, WrT), (OC, WoT[l])):
                    sp.dma_start(w[rows, l, col + E * g:col + E * g + E], part_w).then_inc(S["consts_loaded"], 16)
                with nc.allow_non_contiguous_dma(reason="64 bias values"):
                    sp.dma_start(bq[rows, l:l + 1], bqkv[l, 0:E].rearrange("(e o) -> e o", o=1)).then_inc(S["consts_loaded"], 16)
                    sp.dma_start(bk[rows, l:l + 1], bqkv[l, E:2 * E].rearrange("(e o) -> e o", o=1)).then_inc(S["consts_loaded"], 16)
            for a in range(2):
                for g in range(2):
                    for o, src in ((0, bqkv[l, 2 * E:3 * E]), (P, br)):
                        c0 = 256 * a + o + E * g
                        sp.dma_start(bias_f[:, l, 0, c0:c0 + E], src.partition_broadcast(3)).then_inc(S["consts_loaded"], 16)
            for a in range(8):
                sp.dma_start(bias_f[:, l, 1, E * a:E * a + E], bo[l].partition_broadcast(3)).then_inc(S["consts_loaded"], 16)
        with nc.allow_non_contiguous_dma(reason="small constants"):
            for g in range(2):
                rows = slice(E * g, E * g + E)
                sp.dma_start(gam[rows, :], gamma.rearrange("(e o) -> e o", o=1)).then_inc(S["consts_loaded"], 16)
                sp.dma_start(bet[rows, :], beta.rearrange("(e o) -> e o", o=1)).then_inc(S["consts_loaded"], 16)
                sp.dma_start(wf[rows, :], Wf.rearrange("(f e) o -> e (f o)", e=E)).then_inc(S["consts_loaded"], 16)
            sp.dma_start(bfd[:, 0:1], bf.partition_broadcast(P)).then_inc(S["consts_loaded"], 16)
            sp.dma_start(bfd[:, 1:2], bd.partition_broadcast(P)).then_inc(S["consts_loaded"], 16)

        def load_x(b, k):
            i = b % INFLIGHT
            turn = b // BODY
            if k is not 0 or b >= INFLIGHT:
                sp.wait_ge(S["vr_done"], after(b - INFLIGHT, k))
            sp.dma_start(x[i][:], xT_dram[bass.ds((turn + k) * INFLIGHT + i, 1)].rearrange("t p c -> (t p) c")
                         if k is not 0 else xT_dram[turn * INFLIGHT + i]).then_inc(x_loaded[i], 16)

        def stages(m, k):
            n = m + 2
            if live(n) and (n % BODY) < INFLIGHT:
                load_x(n, k)
            if live(m - 1):
                n = m - 1
                i = n % 2
                if n < 2:
                    sp.wait_ge(S["vbd_ready"], 1)
                sp.wait_ge(S["v_ready"], after(n, k))
                sp.dma_start(v_dram[i], v[i][:, :, :, :].rearrange("p e g a -> p (e g a)")).then_inc(v_stored[i], 16)
                sp.wait_ge(v_stored[i], after2(n, k, 16))
                src = v_dram[i].rearrange("(a t) (h c) -> h t a c", a=4, h=H)
                for h in range(H):
                    sp.dma_start(vbd[i][F * h:F * h + F, :, HD * h:HD * h + HD, :].rearrange("t a d c -> t a (d c)"),
                                 src[h]).then_inc(v_loaded[i], 16)

        for b in range(2):
            load_x(b, 0)
        over_slots(sp, stages)
        sp.wait_ge(S["res_step"], 3)
        sp.dma_start(out.rearrange("(p j) o -> p (j o)", j=NJ), res[:]).then_inc(S["out_stored"], 16)
        sp.wait_ge(S["out_stored"], 16)

    n_consts = 16 * (L * (2 * 7 + 8 + 8) + 6 + 2)

    @block.gpsimd
    def _(pool):
        pool.memset(w[:], 0.0).then_inc(S["consts_zeroed"], 1)
        pool.memset(mhalf[:], -0.5).then_inc(S["ones_set"], 1)
        pool.memset(turn[:], 0.0).then_inc(S["ones_set"], 1)
        pool.wait_ge(S["ones_set"], 2)
        pool.wait_ge(S["consts_ready"], 1)

        def stages(m, k):
            if live(m):
                i = m % 2
                pool.wait_ge(S["k_ready"], after(m, k))
                if m >= 2:
                    pool.wait_ge(S["s_done1"], after(m - 2, k))
                pool.tensor_tensor(turn[:], turn[:], turn[:], ALU.mult).then_inc(S["kh_turn"], 1)
                for h in range(H):
                    last = pool.tensor_scalar(kh[i][:, :, h, :], kt[:].rearrange("p (a f) -> p a f", f=F),
                                              hmask[:, h:h + 1], 1.0, ALU.mult, ALU.mult)
                last.then_inc(S["kh_ready"], 1)
            if live(m - 3):
                pool.wait_ge(S["var_ready"], after(m - 3, k))
                pool.tensor_tensor(rstd[:], var[:], mhalf[:], ALU.pow).then_inc(S["rstd_ready"], 1)

        over_slots(pool, stages)

    @block.scalar
    def _(act):
        act.wait_ge(S["consts_ready"], 1)

        def stages(m, k):
            if live(m - 1):
                n = m - 1
                act.wait_ge(S["vr_done"], after(n, k))
                if n >= 2:
                    act.wait_ge(v_stored[n % 2], after2(n - 2, k, 16))
                    act.wait_ge(S["pv_done"], after(n - 2, k))
                for a in range(2):
                    last = act.activation(v[n % 2][:, :, :, 2 * a:2 * a + 2].rearrange("p e g a -> p a g e"),
                                          bank[2 + a][:, :].rearrange("p (a c) -> p a c", a=2)[:, :, 0:P]
                                          .rearrange("p a (g e) -> p a g e", g=2), ACT.Copy)
                last.then_inc(S["v_ready"], 1)
                if n >= 4:
                    act.wait_ge(S["y_sum_ready"], after(n - 4, k))
                for a in range(2):
                    last = act.activation(r[n % 4][:, 2 * a:2 * a + 2, :],
                                          bank[2 + a][:, :].rearrange("p (a c) -> p a c", a=2)[:, :, P:2 * P], ACT.Relu)
                last.then_inc(S["r_ready"], 1)
            if live(m - 4):
                n = m - 4
                act.wait_ge(S["xt_done"], after(n, k))
                if n % BODY // INFLIGHT == L - 1:
                    act.wait_ge(S["xw_ready"], 1 + INFLIGHT * (n // BODY + k) + n % INFLIGHT)
                    dst = xf[n % 2][:, :, :].rearrange("p a f -> p (a f)")
                else:
                    dst = x[n % INFLIGHT][:]
                act.activation(dst, bank[1][:, :], ACT.Identity, bias=bet[:, 0:1], scale=gam[:, 0:1]).then_inc(S["x_ready"], 1)
            if live(m - 1):
                exp(m - 1, k, 0)
            if live(m - 3):
                act.wait_ge(S["ot_done"], after(m - 3, k))
                if m >= 4:
                    act.wait_ge(S["o_done"], after(m - 4, k))
                act.activation(ot[:], bank[0][:, :], ACT.Copy).then_inc(S["ot_ready"], 1)
            if live(m - 1):
                exp(m - 1, k, 1)
            if live(m):
                l = m % BODY // INFLIGHT
                act.wait_ge(S["k_done"], after(m, k))
                if m >= 1:
                    act.wait_ge(S["kh_ready"], after(m - 1, k))
                act.activation(kt[:], bank[1][:, :], ACT.Identity, bias=bk[:, l:l + 1]).then_inc(S["k_ready"], 1)
                act.wait_ge(S["q_done"], after(m, k))
                if m >= 2:
                    act.wait_ge(S["s_done1"], after(m - 2, k))
                for g in range(2):
                    last = act.activation(qg[m % 2][:, :, g, :], bank[0][:, :].rearrange("p (a f) -> p a f", f=F),
                                          ACT.Identity, bias=bqm[:, l, g:g + 1], scale=qmask[:, g:g + 1])
                last.then_inc(S["q_ready"], 1)
            if live(m - 1):
                turned(m - 1, k, 0)
            if live(m - 3):
                act.wait_ge(S["cen_ready"], after(m - 3, k))
                if m >= 4:
                    act.wait_ge(S["sqs_ready"], after(m - 4, k))
                act.activation(sq[:, :, :], cen[:, :, :], ACT.Square).then_inc(S["sq_ready"], 1)
            if live(m - 1):
                turned(m - 1, k, 1)

        def exp(n, k, a):
            act.wait_ge(S[f"s_sub{a}"], after(n, k))
            if n >= 1:
                act.wait_ge(S[f"pt_turned{a}"], after(n - 1, k))
            act.activation(pr[:, a, :], s[:, a, :, :].rearrange("p a b -> p (a b)"), ACT.Exp).then_inc(S[f"exp_done{a}"], 1)

        def turned(n, k, a):
            act.wait_ge(S[f"pt_turned{a}"], after(n, k))
            if n >= 2 and a == 0:
                act.wait_ge(S["pv_done"], after(n - 2, k))
            act.activation(pt[n % 2][:, a, :], bank[4 + a][:, :], ACT.Copy).then_inc(S[f"pt_ready{a}"], 1)

        over_slots(act, stages)

    @block.vector
    def _(dve):
        for i in range(2):
            dve.memset(vbd[i][:, :, :, :], 0.0).then_inc(S["vbd_zeroed"], 1)
        dve.wait_ge(S["vbd_zeroed"], 2)
        for i in range(2):
            for h in range(H):
                last = dve.memset(vbd[i][F * h:F * h + F, :, E + h:E + h + 1, :], 1.0)
        last.then_inc(S["vbd_ready"], 1)
        dve.tensor_reduce(gmask[:], ident[:].rearrange("p (g c) -> p g c", g=2), AX.X, ALU.add).then_inc(S["bias_step"], 1)
        dve.tensor_reduce(hmask[:], ident[:].rearrange("p (g h d) -> p h g d", g=2, h=H), AX.XY, ALU.add).then_inc(S["bias_step"], 1)
        dve.memset(ones3[:], 1.0).then_inc(S["bias_step"], 1)
        dve.wait_ge(S["consts_loaded"], n_consts)
        dve.wait_ge(S["bias_step"], 3)
        dve.tensor_scalar(qmask[:], gmask[:], SCALE, None, ALU.mult).then_inc(S["bias_step"], 1)
        dve.wait_ge(S["bias_step"], 4)
        for g in range(2):
            dve.tensor_scalar(bqm[:, :, g], bq[:], qmask[:, g:g + 1], None, ALU.mult).then_inc(S["bias_step"], 1)
        dve.tensor_copy(part[0][:], bias_f[:]).then_inc(S["bias_step"], 1)
        dve.wait_ge(S["bias_step"], 7)
        dve.tensor_tensor(bias_t[:], bias_f[:], part[0][:], ALU.subtract).then_inc(S["bias_step"], 1)
        dve.wait_ge(S["bias_step"], 8)
        dve.tensor_copy(part[1][:], bias_t[:]).then_inc(S["bias_step"], 1)
        dve.wait_ge(S["bias_step"], 9)
        dve.tensor_tensor(part[2][:], bias_t[:], part[1][:], ALU.subtract).then_inc(S["bias_step"], 1)
        dve.tensor_scalar(bias3[:], part[0][:], ident[0:3, 0:1], None, ALU.mult).then_inc(S["bias_step"], 1)
        for i in range(1, 3):
            dve.wait_ge(S["bias_step"], 10 + i)
            dve.scalar_tensor_tensor(bias3[:].rearrange("p l a c -> p (l a c)"),
                                     part[i][:].rearrange("p l a c -> p (l a c)"), ident[0:3, i:i + 1],
                                     bias3[:].rearrange("p l a c -> p (l a c)"),
                                     ALU.mult, ALU.add).then_inc(S["bias_step"], 1)
        dve.wait_ge(S["bias_step"], 13)
        for i in range(2):
            dve.memset(xf[i][:], 0.0).then_inc(S["xw_ready"], 1)
        dve.memset(rden[:], 0.0).then_inc(S["z_ready"], 1)
        dve.memset(z[:], 0.0).then_inc(S["consts_ready"], 1)
        dve.wait_ge(S["consts_ready"], 1)

        def maximum(n, k, a):
            dve.wait_ge(S[f"s_done{a}"], after(n, k))
            scores = bank[4 + a][:, :].rearrange("p (a b) -> p a b", b=F)
            dve.tensor_reduce(smax[:, a, :], scores, AX.X, ALU.max).then_inc(S["max_step"], 1)
            dve.wait_ge(S["max_step"], after(n, k, 2) - 1 + a)
            if n >= 1:
                dve.wait_ge(S[f"exp_done{a}"], after(n - 1, k))
            dve.tensor_tensor(s[:, a, :, :], scores,
                              smax[:, a, :].rearrange("p (a o) -> p a o", o=1).to_broadcast([P, PAIRS, F]),
                              ALU.subtract).then_inc(S[f"s_sub{a}"], 1)

        def logit(n, k):
            t = INFLIGHT * (n // BODY + k) + n % INFLIGHT
            dve.wait_ge(S["x_ready"], after(n, k))
            dve.wait_ge(S["z_ready"], t + 1)
            dve.tensor_tensor(xw[:], xf[n % 2][:], wf[:].rearrange("p (o f) -> p o f", o=1).to_broadcast([P, PAIRS, F]),
                              ALU.mult).then_inc(S["xw_ready"], 1)
            dve.wait_ge(S["xw_ready"], t + 3)
            cols = bass.ds(t * PAIRS, PAIRS) if k is not 0 else slice(t * PAIRS, (t + 1) * PAIRS)
            dve.tensor_reduce(z[:, cols], xw[:], AX.X, ALU.add).then_inc(S["z_ready"], 1)

        def stages(m, k):
            if live(m - 4):
                n = m - 4
                dve.wait_ge(S["rstd_ready"], after(n, k))
                if n >= 1:
                    dve.wait_ge(S["xt_done"], after(n - 1, k))
                dve.tensor_tensor(xn[:], cen[:], rstd[:].rearrange("p (a o) -> p a o", o=1).to_broadcast([P, 2 * PQ, E]),
                                  ALU.mult).then_inc(S["xn_ready"], 1)
            if live(m - 1):
                maximum(m - 1, k, 0)
                maximum(m - 1, k, 1)
            if live(m - 2):
                n = m - 2
                dve.wait_ge(S["pv_done"], after(n, k))
                if n >= 1:
                    dve.wait_ge(S["ot_done"], after(n - 1, k))
                for a in range(2):
                    last = dve.reciprocal(rden[:, PQ * a:PQ * a + PQ, :],
                                          bank[6 + a][:, 0:4 * VC].rearrange("p (a c) -> p a c", a=4)[:, :, E:VC])
                last.then_inc(S["rden_ready"], 1)
                dve.wait_ge(S["rden_ready"], after(n, k))
                for a in range(2):
                    last = dve.tensor_tensor(
                        on[:, PQ * a:PQ * a + PQ, :].rearrange("p a (h d) -> p a h d", h=H),
                        bank[6 + a][:, 0:4 * VC].rearrange("p (a c) -> p a c", a=4)[:, :, 0:E]
                        .rearrange("p a (h d) -> p a h d", h=H),
                        rden[:, PQ * a:PQ * a + PQ, :].rearrange("p a (h o) -> p a h o", o=1).to_broadcast([P, PQ, H, HD]),
                        ALU.mult)
                last.then_inc(S["on_ready"], 1)
            if live(m - 3):
                n = m - 3
                dve.wait_ge(S["o_done"], after(n, k))
                dve.wait_ge(S["r_ready"], after(n, k))
                dve.tensor_tensor(y[:].rearrange("p a e -> p (a e)"), bank[0][:, :],
                                  r[n % 4][:].rearrange("p a c -> p (a c)"), ALU.add).then_inc(S["y_sum_ready"], 1)
                dve.wait_ge(S["y_sum_ready"], after(n, k))
                dve.tensor_scalar(y[:], y[:], 0.0, None, ALU.max).then_inc(S["y_ready"], 1)
                dve.wait_ge(S["y_ready"], after(n, k))
                dve.tensor_reduce(ysum[:], y[:], AX.X, ALU.add).then_inc(S["ysum_ready"], 1)
                dve.wait_ge(S["ysum_ready"], after(n, k))
                dve.scalar_tensor_tensor(cen[:], ysum[:].rearrange("p (a o) -> p a o", o=1).to_broadcast([P, 2 * PQ, E]),
                                         -1.0 / E, y[:], ALU.mult, ALU.add).then_inc(S["cen_ready"], 1)
            if live(m - 5) and (m - 5) % BODY // INFLIGHT == L - 1:
                logit(m - 5, k)
            if live(m - 3):
                n = m - 3
                dve.wait_ge(S["sq_ready"], after(n, k))
                dve.tensor_reduce(sqs[:], sq[:], AX.X, ALU.add).then_inc(S["sqs_ready"], 1)
                dve.wait_ge(S["sqs_ready"], after(n, k))
                if n >= 1:
                    dve.wait_ge(S["rstd_ready"], after(n - 1, k))
                dve.tensor_scalar(var[:], sqs[:], 1.0 / E, EPS, ALU.mult, ALU.add).then_inc(S["var_ready"], 1)

        over_slots(dve, stages)
        logit(SLOTS - 1, 0)
        dve.wait_ge(S["att_done"], 1)
        dve.tensor_tensor(res[:], bank[2][:, 0:NJ], dnn[:], ALU.add).then_inc(S["res_step"], 1)
        for i in range(2):
            dve.wait_ge(S["res_step"], i + 1)
            dve.tensor_scalar(res[:], res[:], bfd[:, i:i + 1], None, ALU.add).then_inc(S["res_step"], 1)

    @block.tensor
    def _(pe):
        pe.wait_ge(S["consts_ready"], 1)

        def stages(m, k):
            if live(m - 1):
                n = m - 1
                pe.wait_ge(S["q_ready"], after(n, k))
                pe.wait_ge(S["kh_ready"], after(n, k))
                for a in range(2):
                    if n >= 1:
                        pe.wait_ge(S[f"pt_ready{a}"], after(n - 1, k))
                    for i in range(8):
                        pair = 8 * a + i
                        last = pe.matmul(bank[4 + a][E * (i % 2):E * (i % 2) + E, P * (i // 2):P * (i // 2) + P],
                                         qg[n % 2][:, pair, :, :], kh[n % 2][:, pair, :, :], start=True, stop=True)
                    last.then_inc(S[f"s_done{a}"], 1)
            if live(m - 4):
                n = m - 4
                pe.wait_ge(S["xn_ready"], after(n, k))
                if m - 1 < SLOTS:
                    pe.wait_ge(S["k_ready"], after(m - 1, k))
                elif n >= 1:
                    pe.wait_ge(S["x_ready"], after(n - 1, k))
                for a in range(PQ):
                    last = pe.transpose(bank[1][:, P * a:P * a + P], xn[:, 2 * a:2 * a + 2, :], ident[:])
                last.then_inc(S["xt_done"], 1)
            if live(m - 3):
                n = m - 3
                pe.wait_ge(S["on_ready"], after(n, k))
                if m - 1 < SLOTS:
                    pe.wait_ge(S["q_ready"], after(m - 1, k))
                else:
                    pe.wait_ge(S["y_sum_ready"], after(n - 1, k))
                for a in range(PQ):
                    last = pe.transpose(bank[0][:, P * a:P * a + P], on[:, 2 * a:2 * a + 2, :], ident[:])
                last.then_inc(S["ot_done"], 1)
            if live(m - 2):
                n = m - 2
                pe.wait_ge(S["pt_ready0"], after(n, k))
                pe.wait_ge(S["pt_ready1"], after(n, k))
                pe.wait_ge(v_loaded[n % 2], after2(n, k, 64))
                if n >= 1:
                    pe.wait_ge(S["on_ready"], after(n - 1, k))
                for a in range(PQ):
                    for p4 in range(4):
                        pair = 4 * a + p4
                        for g in range(2):
                            c = VC * (2 * (a % 2) + g)
                            i = 2 * pair + g
                            last = pe.matmul(bank[6 + a // 2][F * p4:F * p4 + F, c:c + VC],
                                             pt[n % 2][:, i // 16, F * (i % 16):F * (i % 16) + F],
                                             vbd[n % 2][:, p4, :, PQ * g + a], start=True, stop=True)
                last.then_inc(S["pv_done"], 1)
            if live(m - 3):
                n = m - 3
                ln = n % BODY // INFLIGHT
                pe.wait_ge(S["ot_ready"], after(n, k))
                for a in range(PQ):
                    pe.matmul(bank[0][:, P * a:P * a + P], ones3[:], bias3[:, ln, 1, P * a:P * a + P],
                              start=True, stop=False)
                    last = pe.matmul(bank[0][:, P * a:P * a + P], ot[:, P * a:P * a + P], w[:, ln, OC:OC + P],
                                     start=False, stop=True)
                last.then_inc(S["o_done"], 1)
            if live(m):
                l = m % BODY // INFLIGHT
                xs = x[m % INFLIGHT]
                if l == 0:
                    pe.wait_ge(x_loaded[m % INFLIGHT], 16 * (m // BODY + 1 + k))
                if m >= 4:
                    pe.wait_ge(S["x_ready"], after(m - 4, k))
                elif m >= 1:
                    pe.wait_ge(S["k_ready"], after(m - 1, k))
                pe.matmul(bank[1][:, :], w[:, l, KCOL:KCOL + P], xs[:], start=True, stop=True).then_inc(S["k_done"], 1)
                if m >= 3:
                    pe.wait_ge(S["y_sum_ready"], after(m - 3, k))
                elif m >= 1:
                    pe.wait_ge(S["q_ready"], after(m - 1, k))
                pe.matmul(bank[0][:, :], w[:, l, QC:QC + P], xs[:], start=True, stop=True).then_inc(S["q_done"], 1)
            if live(m - 1):
                n = m - 1
                for a in range(2):
                    pe.wait_ge(S[f"exp_done{a}"], after(n, k))
                    for i in range(4):
                        last = pe.transpose(bank[4 + a][:, P * i:P * i + P], pr[:, a, P * i:P * i + P], ident[:])
                    last.then_inc(S[f"pt_turned{a}"], 1)
            if live(m):
                if m >= 1:
                    pe.wait_ge(S["r_ready"], after(m - 1, k))
                for n in range(2):
                    for a in range(2):
                        c = P * (2 * n + a)
                        pe.matmul(bank[2 + n][:, 256 * a:256 * a + 256], ones3[:],
                                  bias3[:, l, 0, 256 * a:256 * a + 256], start=True, stop=False)
                        last = pe.matmul(bank[2 + n][:, 256 * a:256 * a + 256], xs[:, c:c + P],
                                         w[:, l, VR:VR + 256], start=False, stop=True)
                last.then_inc(S["vr_done"], 1)

        over_slots(pe, stages)
        pe.wait_ge(S["z_ready"], NT + 1)
        for d in range(NDG):
            last = pe.matmul(bank[2][:, 2 * d:2 * d + 2], z[:, P * d:P * d + P], gmask[:], start=True, stop=True)
        last.then_inc(S["att_done"], 1)


def kernel(**inputs):
    import numpy as np
    import concourse.bacc as bacc
    from concourse.bass_utils import run_bass_kernel_spmd as run

    def n(name):
        return np.asarray(inputs["L0_rec_" + name])

    arrays = {
        "Xi": np.ascontiguousarray(inputs["r_Xi"]),
        "Xv": n("Xv"), "tables": n("tables"),
        "WqkvT": np.ascontiguousarray(n("Wqkv").transpose(0, 2, 1)),
        "bqkv": n("bqkv"),
        "WoT": np.ascontiguousarray(n("Wo").transpose(0, 2, 1)),
        "bo": n("bo"),
        "WrT": np.ascontiguousarray(n("Wr").T),
        "br": n("br"), "gamma": n("gamma"), "beta": n("beta"),
        "Wf": n("Wf"), "bf": n("bf"), "W1": n("W1"), "b1": n("b1"),
        "W2": n("W2"), "b2": n("b2"), "Wd": n("Wd"), "bd": n("bd"),
        "ident": np.eye(P, dtype=np.float32),
    }
    nc = bacc.Bacc("TRN2", target_bir_lowering=False, num_devices=1)
    args = [nc.dram_tensor(f"in_{k}", a.shape, mybir.dt.from_np(a.dtype), kind="ExternalInput").ap()
            for k, a in arrays.items()]
    args.append(nc.dram_tensor("out_y", (B, 1), F32, kind="ExternalOutput").ap())
    build(nc, *args)
    r = run(nc, [{f"in_{k}": a for k, a in arrays.items()}], core_ids=[0])
    return r.results[0]["out_y"]
```

```python
from contextlib import ExitStack

import concourse.bass as bass
from concourse import mybir

F32 = mybir.dt.float32
BF16 = mybir.dt.bfloat16
I32 = mybir.dt.int32
ALU = mybir.AluOpType
ACT = mybir.ActivationFunctionType
AX = mybir.AxisListType

B, F, V, E, H, L = 2048, 32, 6250, 64, 4, 3
HD = E // H
D1, D2 = 1024, 512
P = 128
NJ = B // P
NDG = NJ // 2
PAIRS = 16
TOK = PAIRS * F
NT = B // (2 * PAIRS)
PB = P // PAIRS
PQ = PAIRS // 4
SLOTS = NT * L
INFLIGHT = 4
BODY = INFLIGHT * L
LEAD = 5
TURNS = (SLOTS - LEAD) // BODY
KC = F * E // P
KC2 = D1 // P
EPS = 1e-5
SCALE = 1.0 / float(HD) ** 0.5
VC = E + H


def build(nc, Xi, Xv, tables, WqkvT, bqkv, WoT, bo, WrT, br, gamma, beta, Wf, bf,
          W1, b1, W2, b2, Wd, bd, ident_in, out):
    xT_dram = nc.dram_tensor("xT_scratch", (NT, P, TOK), F32, kind="Internal").ap()
    v_dram = nc.dram_tensor("v_scratch", (2, P, TOK), F32, kind="Internal").ap()
    with ExitStack() as ctx:
        def sb(name, shape, dt=F32, to=ctx):
            return to.enter_context(nc.sbuf_tensor(name, shape, dt))

        def sem(name):
            return ctx.enter_context(nc.semaphore(name))

        bank = [ctx.enter_context(nc.psum_tensor(f"bank{i}", [P, 512], F32)) for i in range(8)]
        C = {
            "ident": sb("ident", [P, P]),
            "dnn": sb("dnn", [P, NJ]),
            "w": sb("w", [P, L, 5 * P]),
            "bq": sb("bq", [P, L]),
            "bk": sb("bk", [P, L]),
            "bqm": sb("bqm", [P, L, 2]),
            "gmask": sb("gmask", [P, 2]),
            "qmask": sb("qmask", [P, 2]),
            "hmask": sb("hmask", [P, H]),
            "gam": sb("gam", [P, 1]),
            "bet": sb("bet", [P, 1]),
            "wf": sb("wf", [P, F]),
            "bfd": sb("bfd", [P, 2]),
            "ones3": sb("ones3", [3, P], BF16),
            "bias3": sb("bias3", [3, L, 2, P], BF16),
            "mhalf": sb("mhalf", [P, 2 * PQ]),
        }
        phase_one(nc, sb, sem, bank, C, xT_dram, Xi, Xv, tables, WqkvT, bqkv, WoT, bo, WrT, br,
                  gamma, beta, Wf, bf, W1, b1, W2, b2, Wd, bd, ident_in)
        phase_two(nc, ctx, sb, sem, bank, C, xT_dram, v_dram, out)


def phase_one(nc, sb, sem, bank, C, xT_dram, Xi, Xv, tables, WqkvT, bqkv, WoT, bo, WrT, br,
              gamma, beta, Wf, bf, W1, b1, W2, b2, Wd, bd, ident_in):
    ident, dnn, w, ones3, bias3 = (C[x] for x in ("ident", "dnn", "w", "ones3", "bias3"))
    with ExitStack() as ph:
        def s1(name, shape, dt=F32):
            return sb(name, shape, dt, ph)

        w1 = s1("w1", [P, KC, D1])
        w2 = s1("w2", [P, KC2, D2])
        wd_b = s1("wd_b", [P, D2])
        bias_m = s1("bias_m", [3, D1 + D2])
        bias_m3 = s1("bias_m3", [3, D1 + D2], BF16)
        bias_a = s1("bias_a", [3, L, 2, P])
        keep = s1("keep", [3, 2])
        bv = s1("bv", [P, L])
        bv3 = s1("bv3", [P, L, 3])
        xi = s1("xi", [P, NJ * F], I32)
        neg = s1("neg", [P, NJ * F], I32)
        base = s1("base", [P, F], I32)
        xv = s1("xv", [P, NJ * F])
        idx = [s1(f"idx{u}", [P, F], I32) for u in range(2)]
        emb = [s1(f"emb{u}", [P, F, E]) for u in range(2)]
        pairs = s1("pairs", [P, F, E, 2])
        xt = s1("xt", [P, P, F])
        et = [s1(f"et{g}", [P, KC, P]) for g in range(2)]
        turn = s1("turn", [1, 1])
        h1 = [s1(f"h1_{u}", [P, D1]) for u in range(2)]
        h1t = s1("h1t", [P, KC2, P])
        h2 = s1("h2", [P, D2])
        h2w = s1("h2w", [P, D2])
        logit = s1("logit", [P, 1])

        xi_loaded = sem("xi_loaded")
        setup_loaded = sem("setup_loaded")
        b_loaded = sem("b_loaded")
        W1_PARTS = 4
        w1_loaded = [sem(f"w1_loaded{i}") for i in range(W1_PARTS)]
        w2_loaded = sem("w2_loaded")
        consts_zeroed = sem("consts_zeroed")
        consts_loaded = sem("consts_loaded")
        base_ready = sem("base_ready")
        idx_all = sem("idx_all")
        idx_cur = sem("idx_cur")
        gather_turn = sem("gather_turn")
        gathered = [sem(f"gathered{u}") for u in range(2)]
        prep = sem("prep")
        mlp_bias = sem("mlp_bias")
        att_prep = sem("att_prep")
        bv_ready = sem("bv_ready")
        bv_done = sem("bv_done")
        scaled = sem("scaled")
        et_turned = sem("et_turned")
        et_copied = sem("et_copied")
        xt_turned = sem("xt_turned")
        xt_copied = sem("xt_copied")
        xt_stored = sem("xt_stored")
        h1_done = sem("h1_done")
        h1_relu = sem("h1_relu")
        h1t_turned = sem("h1t_turned")
        h1t_copied = sem("h1t_copied")
        h2_done = sem("h2_done")
        h2_relu = sem("h2_relu")
        dnn_done = sem("dnn_done")
        dnn_stored = sem("dnn_stored")
        QC, KCOL, VCOL, RC, OC = (i * P for i in range(5))

        block = ph.enter_context(nc.Block())

        def over_steps(eng, step, first, stop):
            for j in range(first, 2):
                step(j, j % 2, j // 2)
            turns = (min(stop, NJ - 1) - 2) // 2
            with eng.Fori(0, turns) as k:
                for g in range(2):
                    step(2 * k + 2 + g, g, k + 1)
            for j in range(2 + 2 * turns, stop):
                step(j, j % 2, j // 2)

        @block.sync
        def _(sp):
            sp.dma_start(xi[:], Xi.rearrange("(p j) f -> p (j f)", j=NJ)).then_inc(xi_loaded, 16)
            sp.dma_start(ident[:], ident_in).then_inc(setup_loaded, 16)
            sp.dma_start(xv[:], Xv.rearrange("(p j) f o -> p (j f o)", j=NJ)).then_inc(setup_loaded, 16)
            sp.dma_start(bias_m[:, 0:D1], b1.partition_broadcast(3)).then_inc(b_loaded, 16)
            sp.dma_start(bias_m[:, D1:D1 + D2], b2.partition_broadcast(3)).then_inc(b_loaded, 16)
            for i in range(W1_PARTS):
                c = slice(i * KC // W1_PARTS, (i + 1) * KC // W1_PARTS)
                sp.dma_start(w1[:, c, :], W1.rearrange("(c p) n -> p c n", p=P)[:, c, :]).then_inc(w1_loaded[i], 16)
            sp.dma_start(w2[:], W2.rearrange("(c p) n -> p c n", p=P)).then_inc(w2_loaded, 16)
            sp.dma_start(wd_b[:], Wd.rearrange("n o -> (n o)").partition_broadcast(P)).then_inc(w2_loaded, 16)
            sp.wait_ge(consts_zeroed, 1)
            for l in range(L):
                for g in range(2):
                    rows = slice(E * g, E * g + E)
                    for col, part_w in ((QC, WqkvT[l, :, 0:E]), (KCOL, WqkvT[l, :, E:2 * E]),
                                        (VCOL, WqkvT[l, :, 2 * E:3 * E]), (RC, WrT), (OC, WoT[l])):
                        sp.dma_start(w[rows, l, col + E * g:col + E * g + E], part_w).then_inc(consts_loaded, 16)
                    with nc.allow_non_contiguous_dma(reason="64 bias values"):
                        for b, at in ((C["bq"], 0), (C["bk"], E), (bv, 2 * E)):
                            sp.dma_start(b[rows, l:l + 1], bqkv[l, at:at + E].rearrange("(e o) -> e o", o=1)
                                         ).then_inc(consts_loaded, 16)
                    sp.dma_start(bias_a[:, l, 0, rows], br.partition_broadcast(3)).then_inc(consts_loaded, 16)
                    sp.dma_start(bias_a[:, l, 1, rows], bo[l].partition_broadcast(3)).then_inc(consts_loaded, 16)
            with nc.allow_non_contiguous_dma(reason="small constants"):
                for g in range(2):
                    rows = slice(E * g, E * g + E)
                    sp.dma_start(C["gam"][rows, :], gamma.rearrange("(e o) -> e o", o=1)).then_inc(consts_loaded, 16)
                    sp.dma_start(C["bet"][rows, :], beta.rearrange("(e o) -> e o", o=1)).then_inc(consts_loaded, 16)
                    sp.dma_start(C["wf"][rows, :], Wf.rearrange("(f e) o -> e (f o)", e=E)).then_inc(consts_loaded, 16)
                sp.dma_start(C["bfd"][:, 0:1], bf.partition_broadcast(P)).then_inc(consts_loaded, 16)
                sp.dma_start(C["bfd"][:, 1:2], bd.partition_broadcast(P)).then_inc(consts_loaded, 16)
            with sp.Fori(0, NDG) as d:
                sp.wait_ge(xt_copied, 8 * d + 8)
                for g in range(2):
                    sp.dma_start(xT_dram[bass.ds(d * PB, PB), E * g:E * g + E].rearrange("t p c -> p t c"),
                                 xt[g:P:2, :, :].rearrange("p (t a) f -> p t (a f)", t=PB)).then_inc(xt_stored, 16)
            sp.wait_ge(xt_stored, 32 * NDG)

        n_consts = 16 * (L * 2 * 10 + 6 + 2)

        @block.gpsimd
        def _(pool):
            pool.iota(base[:], [[V, F]], base=0, channel_multiplier=0).then_inc(base_ready, 1)
            pool.memset(turn[:], 0.0).then_inc(base_ready, 1)
            pool.memset(C["mhalf"][:], -0.5).then_inc(base_ready, 1)
            pool.wait_ge(base_ready, 3)
            pool.wait_ge(idx_all, 4)
            rows = tables.rearrange("f v e -> (f v) e")

            def step(j, g, half):
                if half is not 0:
                    pool.wait_ge(gathered[g], 16 * F * half)
                    pool.wait_ge(scaled, j - 1)
                pool.tensor_copy(idx[g][:], xi[:, bass.ds(j * F, F)] if half is not 0
                                 else xi[:, j * F:j * F + F]).then_inc(idx_cur, 1)
                pool.wait_ge(idx_cur, j + 1)
                pool.tensor_tensor(turn[:], turn[:], turn[:], ALU.mult).then_inc(gather_turn, 1)
                for f in range(F):
                    pool.indirect_dma_start(emb[g][:, f, :], None, rows,
                                            bass.IndirectOffsetOnAxis(idx[g][:, f:f + 1], 0)
                                            ).then_inc(gathered[g], 16)

            over_steps(pool, step, 0, NJ)

        @block.vector
        def _(dve):
            dve.memset(ones3[:], 1.0).then_inc(prep, 1)
            dve.memset(w[:], 0.0).then_inc(consts_zeroed, 1)
            dve.wait_ge(xi_loaded, 16)
            dve.tensor_scalar(neg[:], xi[:], 0.0, float(V), ALU.is_lt, ALU.mult).then_inc(idx_all, 1)
            dve.wait_ge(idx_all, 1)
            dve.tensor_tensor(neg[:], xi[:], neg[:], ALU.add).then_inc(idx_all, 1)
            dve.wait_ge(idx_all, 2)
            dve.tensor_scalar(neg[:], neg[:], float(V - 1), 0.0, ALU.min, ALU.max).then_inc(idx_all, 1)
            dve.wait_ge(idx_all, 3)
            dve.wait_ge(base_ready, 3)
            dve.tensor_tensor(xi[:].rearrange("p (j f) -> p j f", f=F), neg[:].rearrange("p (j f) -> p j f", f=F),
                              base[:].rearrange("p (o f) -> p o f", o=1).to_broadcast([P, NJ, F]),
                              ALU.add).then_inc(idx_all, 1)
            dve.wait_ge(setup_loaded, 32)
            dve.tensor_scalar(keep[:, 0:1], ident[0:3, 0:1], 1.0, None, ALU.subtract).then_inc(prep, 1)
            dve.tensor_scalar(keep[:, 1:2], ident[0:3, 2:3], -1.0, None, ALU.mult).then_inc(prep, 1)
            dve.wait_ge(prep, 3)
            dve.wait_ge(b_loaded, 32)

            def split(rows, parts, done):
                for i in range(2):
                    dve.tensor_copy(parts, rows).then_inc(done, 1)
                    dve.wait_ge(done, 2 * i + 1)
                    dve.scalar_tensor_tensor(rows, parts, keep[:, i:i + 1], rows, ALU.mult, ALU.add).then_inc(done, 1)
                    dve.wait_ge(done, 2 * i + 2)
                dve.tensor_copy(parts, rows).then_inc(done, 1)

            split(bias_m[:], bias_m3[:], mlp_bias)

            def scale(j, g, half):
                dve.wait_ge(gathered[g], 16 * F * (half + 1))
                if half is not 0:
                    dve.wait_ge(xt_turned, 8 * half)
                xvj = xv[:, bass.ds(j * F, F)] if half is not 0 else xv[:, j * F:j * F + F]
                dve.tensor_tensor(pairs[:, :, :, g], emb[g][:],
                                  xvj.rearrange("p (f o) -> p f o", o=1).to_broadcast([P, F, E]),
                                  ALU.mult).then_inc(scaled, 1)

            def copy_et(j, g, c):
                dve.wait_ge(et_turned, 4 * j + c + 1)
                dve.tensor_copy(et[g][:, 4 * c:4 * c + 4, :],
                                bank[(2, 3, 7, 2)[c]][:, :].rearrange("p (a b) -> p a b", a=4)).then_inc(et_copied, 1)

            def copy_h1t(j, c):
                dve.wait_ge(h1t_turned, 2 * j + c + 1)
                dve.tensor_copy(h1t[:, 4 * c:4 * c + 4, :],
                                bank[(3, 7)[c]][:, :].rearrange("p (a b) -> p a b", a=4)).then_inc(h1t_copied, 1)

            def step(j, g, half):
                more = j is not NJ - 1 and j is not NJ
                if more:
                    scale(j + 1, 1 - g, half + g)
                    for c in range(3):
                        copy_et(j + 1, 1 - g, c)
                if j is not 0:
                    copy_h1t(j - 1, 0)
                if more:
                    copy_et(j + 1, 1 - g, 3)
                if j is not 0:
                    copy_h1t(j - 1, 1)
                    dve.wait_ge(h2_relu, j)
                    dve.tensor_tensor_reduce(h2w[:], h2[:], wd_b[:], 1.0, 0.0, ALU.mult, ALU.add,
                                             logit[:]).then_inc(dnn_done, 1)
                    dve.wait_ge(dnn_done, j)
                    dve.tensor_copy(dnn[:, bass.ds(j - 1, 1)] if not isinstance(j, int) else dnn[:, j - 1:j],
                                    logit[:]).then_inc(dnn_stored, 1)
                    dve.wait_ge(dnn_stored, j)

            scale(0, 0, 0)
            for c in range(4):
                copy_et(0, 0, c)
            dve.wait_ge(w2_loaded, 32)
            over_steps(dve, step, 0, NJ + 1)

            gmask, hmask, qmask = C["gmask"], C["hmask"], C["qmask"]
            dve.wait_ge(consts_loaded, n_consts)
            dve.tensor_copy(bv3[:], bv[:].rearrange("p (l o) -> p l o", o=1).to_broadcast([P, L, 3])).then_inc(bv_ready, 1)
            dve.tensor_reduce(gmask[:], ident[:].rearrange("p (g c) -> p g c", g=2), AX.X, ALU.add).then_inc(prep, 1)
            dve.tensor_reduce(hmask[:], ident[:].rearrange("p (g h d) -> p h g d", g=2, h=H), AX.XY, ALU.add).then_inc(prep, 1)
            dve.wait_ge(prep, 5)
            dve.tensor_scalar(qmask[:], gmask[:], SCALE, None, ALU.mult).then_inc(prep, 1)
            dve.wait_ge(prep, 6)
            for g in range(2):
                dve.tensor_scalar(C["bqm"][:, :, g], C["bq"][:], qmask[:, g:g + 1], None, ALU.mult).then_inc(prep, 1)
            dve.wait_ge(bv_done, 1)
            dve.tensor_tensor(bias_a[:, :, 1, :], bias_a[:, :, 1, :],
                              bank[6][0:3, 0:L * P].rearrange("p (l c) -> p l c", l=L), ALU.add).then_inc(prep, 1)
            dve.wait_ge(prep, 9)
            split(bias_a[:], bias3[:], att_prep)

        @block.scalar
        def _(act):
            def step(j, g, half):
                if j is not NJ:
                    for n in range(2):
                        act.wait_ge(h1_done, 2 * j + n + 1)
                        act.activation(h1[g][:, 512 * n:512 * n + 512], bank[4 + n][:, :],
                                       ACT.Relu).then_inc(h1_relu, 1)
                        if n == 0 and g == 0:
                            if half is not 0:
                                act.wait_ge(xt_stored, 32 * half)
                            for c in range(8):
                                act.wait_ge(xt_turned, 8 * half + c + 1)
                                act.activation(xt[:, :, 4 * c:4 * c + 4].rearrange("p a f -> p f a"),
                                               bank[c % 2][:, :].rearrange("p (f a) -> p f a", f=4),
                                               ACT.Copy).then_inc(xt_copied, 1)
                if j is not 0:
                    act.wait_ge(h2_done, j)
                    if j is not 1:
                        act.wait_ge(dnn_done, j - 1)
                    act.activation(h2[:], bank[6][:, :], ACT.Relu).then_inc(h2_relu, 1)

            over_steps(act, step, 0, NJ + 1)

        @block.tensor
        def _(pe):
            def turn_et(j, g, c):
                for i in range(4):
                    f = 2 * (4 * c + i)
                    last = pe.transpose(bank[(2, 3, 7, 2)[c]][:, P * i:P * i + P],
                                        pairs[:, f:f + 2, :, g].rearrange("p f e -> p (f e)"), ident[:])
                last.then_inc(et_turned, 1)

            def turn_h1(j, g, c):
                for i in range(4):
                    m = 4 * c + i
                    last = pe.transpose(bank[(3, 7)[c]][:, P * i:P * i + P], h1[g][:, P * m:P * m + P], ident[:])
                last.then_inc(h1t_turned, 1)

            def half_h1(j, g, n):
                if j is not 0:
                    pe.wait_ge(h1_relu, 2 * (j - 1) + n + 1)
                cols = slice(512 * n, 512 * n + 512)
                pe.matmul(bank[4 + n][:, :], ones3[:], bias_m3[:, cols], start=True, stop=False)
                for c in range(KC):
                    if j is 0 and n == 0 and c % (KC // W1_PARTS) == 0:
                        pe.wait_ge(w1_loaded[c * W1_PARTS // KC], 16)
                    last = pe.matmul(bank[4 + n][:, :], et[g][:, c, :], w1[:, c, cols],
                                     start=False, stop=(c == KC - 1))
                last.then_inc(h1_done, 1)

            def step(j, g, half):
                more = j is not NJ - 1 and j is not NJ
                if j is not NJ:
                    pe.wait_ge(et_copied, 4 * j + 4)
                    half_h1(j, g, 0)
                if j is not 0 and j is not 1:
                    pe.wait_ge(h1t_copied, 2 * (j - 1))
                if more:
                    pe.wait_ge(scaled, j + 2)
                    for c in range(3):
                        turn_et(j + 1, 1 - g, c)
                if j is not 0:
                    pe.wait_ge(h1_relu, 2 * j)
                    if more:
                        pe.wait_ge(et_copied, 4 * (j + 1) + 2)
                    turn_h1(j - 1, 1 - g, 0)
                if more:
                    pe.wait_ge(et_copied, 4 * (j + 1) + 1)
                    turn_et(j + 1, 1 - g, 3)
                if j is not 0:
                    if more:
                        pe.wait_ge(et_copied, 4 * (j + 1) + 3)
                    turn_h1(j - 1, 1 - g, 1)
                if g == 0 and j is not NJ:
                    for c in range(8):
                        if half is not 0 or c >= 2:
                            pe.wait_ge(xt_copied, 8 * half + c - 1)
                        for i in range(4):
                            last = pe.transpose(bank[c % 2][:, P * i:P * i + P],
                                                pairs[:, 4 * c + i, :, :].rearrange("p e g -> p (e g)"), ident[:])
                        last.then_inc(xt_turned, 1)
                if j is not NJ:
                    half_h1(j, g, 1)
                if j is not 0:
                    if j is not 1:
                        pe.wait_ge(h2_relu, j - 1)
                    else:
                        pe.wait_ge(w2_loaded, 32)
                    pe.matmul(bank[6][:, :], ones3[:], bias_m3[:, D1:D1 + D2], start=True, stop=False)
                    pe.wait_ge(h1t_copied, 2 * j)
                    for c in range(KC2):
                        last = pe.matmul(bank[6][:, :], h1t[:, c, :], w2[:, c, :],
                                         start=False, stop=(c == KC2 - 1))
                    last.then_inc(h2_done, 1)

            pe.wait_ge(setup_loaded, 32)
            pe.wait_ge(scaled, 1)
            for c in range(4):
                if c == 3:
                    pe.wait_ge(et_copied, 1)
                turn_et(0, 0, c)
            pe.wait_ge(mlp_bias, 5)
            over_steps(pe, step, 0, NJ + 1)
            pe.wait_ge(bv_ready, 1)
            pe.wait_ge(h2_relu, NJ)
            for l in range(L):
                last = pe.matmul(bank[6][0:3, P * l:P * l + P], bv3[:, l, :], w[:, l, OC:OC + P], start=True, stop=True)
            last.then_inc(bv_done, 1)


def phase_two(nc, ctx, sb, sem, bank, C, xT_dram, v_dram, out):
    QC, KCOL, VCOL, RC, OC = (i * P for i in range(5))
    ident, dnn, w, bk, bqm, gmask, qmask, hmask, gam, bet, wf, bfd, ones3, bias3, mhalf = (
        C[n] for n in "ident dnn w bk bqm gmask qmask hmask gam bet wf bfd ones3 bias3 mhalf".split())
    turn = sb("turn2", [1, 1])

    x = [sb(f"x{i}", [P, TOK]) for i in range(INFLIGHT)]
    xf = [sb(f"xf{i}", [P, PAIRS, F]) for i in range(2)]
    xw = sb("xw", [P, PAIRS, F])
    z = sb("z", [P, NT * PAIRS])
    kt = sb("kt", [P, TOK])
    qg = [sb(f"qg{i}", [P, PAIRS, 2, F]) for i in range(2)]
    kh = [sb(f"kh{i}", [P, PAIRS, H, F]) for i in range(2)]
    v = [sb(f"v{i}", [P, E, 2, PQ]) for i in range(2)]
    vbd = [sb(f"vbd{i}", [P, 4, VC, 2 * PQ]) for i in range(2)]
    r = [sb(f"r{i}", [P, PQ, P]) for i in range(4)]
    smax = sb("smax", [P, 2, PAIRS])
    s = sb("s", [P, 2, PAIRS, F])
    pr = sb("pr", [P, 2, PAIRS * F])
    pt = [sb(f"pt{i}", [P, 2, PAIRS * F]) for i in range(2)]
    rden = sb("rden", [P, 2 * PQ, H])
    on = sb("on", [P, 2 * PQ, E])
    ot = sb("ot", [P, TOK])
    y = sb("y", [P, 2 * PQ, E])
    ysum = sb("ysum", [P, 2 * PQ])
    cen = sb("cen", [P, 2 * PQ, E])
    sq = sb("sq", [P, 2 * PQ, E])
    sqs = sb("sqs", [P, 2 * PQ])
    var = sb("var", [P, 2 * PQ])
    rstd = sb("rstd", [P, 2 * PQ])
    xn = sb("xn", [P, 2 * PQ, E])
    res = sb("res", [P, NJ])

    names = """turn_ready vbd_zeroed vbd_ready
        k_done q_done v_done r_done s_done0 s_done1 pv_done ot_done o_done xt_done
        k_ready q_ready kh_turn kh_ready r_ready v_ready ot_ready x_ready
        max_step s_sub0 s_sub1 exp_done0 exp_done1 pt_turned0 pt_turned1 pt_ready0 pt_ready1
        rden_ready on_ready y_sum_ready y_ready ysum_ready cen_ready sq_ready sqs_ready var_ready
        rstd_ready xn_ready xw_ready z_ready att_done res_step out_stored""".split()
    S = {n: sem(n) for n in names}
    x_loaded = [sem(f"x_loaded{i}") for i in range(INFLIGHT)]
    v_stored = [sem(f"v_stored{i}") for i in range(2)]
    v_loaded = [sem(f"v_loaded{i}") for i in range(2)]

    def after(b, k, per=1):
        return (b + 1) * per + BODY * per * k

    def after2(b, k, per):
        return (b // 2 + 1) * per + BODY // 2 * per * k

    def over_slots(eng, stages):
        for m in range(LEAD):
            stages(m, 0)
        with eng.Fori(0, TURNS) as k:
            for m in range(LEAD, LEAD + BODY):
                stages(m, k)
        for m in range(LEAD + BODY * TURNS, SLOTS + 4):
            stages(m, 0)

    def over_groups(row):
        return row.rearrange("p (o c) -> p o c", o=1).to_broadcast([3, PQ, P])

    def live(n):
        return 0 <= n < SLOTS

    block = ctx.enter_context(nc.Block())

    @block.sync
    def _(sp):
        def load_x(b, k):
            i = b % INFLIGHT
            turn = b // BODY
            if k is not 0 or b >= INFLIGHT:
                sp.wait_ge(S["r_done"], after(b - INFLIGHT, k))
            sp.dma_start(x[i][:], xT_dram[bass.ds((turn + k) * INFLIGHT + i, 1)].rearrange("t p c -> (t p) c")
                         if k is not 0 else xT_dram[turn * INFLIGHT + i]).then_inc(x_loaded[i], 16)

        def stages(m, k):
            n = m + 2
            if live(n) and (n % BODY) < INFLIGHT:
                load_x(n, k)
            if live(m - 1):
                n = m - 1
                i = n % 2
                if n < 2:
                    sp.wait_ge(S["vbd_ready"], 1)
                sp.wait_ge(S["v_ready"], after(n, k))
                sp.dma_start(v_dram[i], v[i][:, :, :, :].rearrange("p e g a -> p (e g a)")).then_inc(v_stored[i], 16)
                sp.wait_ge(v_stored[i], after2(n, k, 16))
                src = v_dram[i].rearrange("(a t) (h c) -> h t a c", a=4, h=H)
                for h in range(H):
                    sp.dma_start(vbd[i][F * h:F * h + F, :, HD * h:HD * h + HD, :].rearrange("t a d c -> t a (d c)"),
                                 src[h]).then_inc(v_loaded[i], 16)

        for b in range(2):
            load_x(b, 0)
        over_slots(sp, stages)
        sp.wait_ge(S["res_step"], 3)
        sp.dma_start(out.rearrange("(p j) o -> p (j o)", j=NJ), res[:]).then_inc(S["out_stored"], 16)
        sp.wait_ge(S["out_stored"], 16)

    @block.gpsimd
    def _(pool):
        pool.memset(turn[:], 0.0).then_inc(S["turn_ready"], 1)
        pool.wait_ge(S["turn_ready"], 1)

        def stages(m, k):
            if live(m):
                i = m % 2
                pool.wait_ge(S["k_ready"], after(m, k))
                if m >= 2:
                    pool.wait_ge(S["s_done1"], after(m - 2, k))
                pool.tensor_tensor(turn[:], turn[:], turn[:], ALU.mult).then_inc(S["kh_turn"], 1)
                for h in range(H):
                    last = pool.tensor_scalar(kh[i][:, :, h, :], kt[:].rearrange("p (a f) -> p a f", f=F),
                                              hmask[:, h:h + 1], 1.0, ALU.mult, ALU.mult)
                last.then_inc(S["kh_ready"], 1)
            if live(m - 3):
                pool.wait_ge(S["var_ready"], after(m - 3, k))
                pool.tensor_tensor(rstd[:], var[:], mhalf[:], ALU.pow).then_inc(S["rstd_ready"], 1)

        over_slots(pool, stages)

    @block.scalar
    def _(act):
        def stages(m, k):
            if live(m - 1):
                n = m - 1
                act.wait_ge(S["v_done"], after(n, k))
                if n >= 2:
                    act.wait_ge(v_stored[n % 2], after2(n - 2, k, 16))
                    act.wait_ge(S["pv_done"], after(n - 2, k))
                act.activation(v[n % 2][:, :, :, :].rearrange("p e g a -> p a g e"),
                               bank[2][:, :].rearrange("p (a g e) -> p a g e", a=PQ, g=2), ACT.Copy).then_inc(S["v_ready"], 1)
                act.wait_ge(S["r_done"], after(n, k))
                if n >= 4:
                    act.wait_ge(S["y_sum_ready"], after(n - 4, k))
                act.activation(r[n % 4][:].rearrange("p a c -> p (a c)"), bank[3][:, :], ACT.Relu).then_inc(S["r_ready"], 1)
            if live(m - 3):
                act.wait_ge(S["ot_done"], after(m - 3, k))
                if m >= 4:
                    act.wait_ge(S["o_done"], after(m - 4, k))
                act.activation(ot[:], bank[0][:, :], ACT.Copy).then_inc(S["ot_ready"], 1)
            if live(m - 1):
                exp(m - 1, k, 0)
            if live(m - 4):
                n = m - 4
                act.wait_ge(S["xt_done"], after(n, k))
                if n % BODY // INFLIGHT == L - 1:
                    act.wait_ge(S["xw_ready"], 1 + INFLIGHT * (n // BODY + k) + n % INFLIGHT)
                    dst = xf[n % 2][:, :, :].rearrange("p a f -> p (a f)")
                else:
                    dst = x[n % INFLIGHT][:]
                act.activation(dst, bank[1][:, :], ACT.Identity, bias=bet[:, 0:1], scale=gam[:, 0:1]).then_inc(S["x_ready"], 1)
            if live(m - 1):
                exp(m - 1, k, 1)
            if live(m):
                l = m % BODY // INFLIGHT
                act.wait_ge(S["k_done"], after(m, k))
                if m >= 1:
                    act.wait_ge(S["kh_ready"], after(m - 1, k))
                act.activation(kt[:], bank[1][:, :], ACT.Identity, bias=bk[:, l:l + 1]).then_inc(S["k_ready"], 1)
                act.wait_ge(S["q_done"], after(m, k))
                if m >= 2:
                    act.wait_ge(S["s_done1"], after(m - 2, k))
                for g in range(2):
                    last = act.activation(qg[m % 2][:, :, g, :], bank[0][:, :].rearrange("p (a f) -> p a f", f=F),
                                          ACT.Identity, bias=bqm[:, l, g:g + 1], scale=qmask[:, g:g + 1])
                last.then_inc(S["q_ready"], 1)
            if live(m - 3):
                act.wait_ge(S["cen_ready"], after(m - 3, k))
                if m >= 4:
                    act.wait_ge(S["sqs_ready"], after(m - 4, k))
                act.activation(sq[:, :, :], cen[:, :, :], ACT.Square).then_inc(S["sq_ready"], 1)
            if live(m - 1):
                turned(m - 1, k, 0)
                turned(m - 1, k, 1)

        def exp(n, k, a):
            act.wait_ge(S[f"s_sub{a}"], after(n, k))
            if n >= 1:
                act.wait_ge(S[f"pt_turned{a}"], after(n - 1, k))
            act.activation(pr[:, a, :], s[:, a, :, :].rearrange("p a b -> p (a b)"), ACT.Exp).then_inc(S[f"exp_done{a}"], 1)

        def turned(n, k, a):
            act.wait_ge(S[f"pt_turned{a}"], after(n, k))
            if n >= 2 and a == 0:
                act.wait_ge(S["pv_done"], after(n - 2, k))
            act.activation(pt[n % 2][:, a, :], bank[4 + a][:, :], ACT.Copy).then_inc(S[f"pt_ready{a}"], 1)

        over_slots(act, stages)

    @block.vector
    def _(dve):
        for i in range(2):
            dve.memset(vbd[i][:, :, :, :], 0.0).then_inc(S["vbd_zeroed"], 1)
        dve.wait_ge(S["vbd_zeroed"], 2)
        for i in range(2):
            for h in range(H):
                last = dve.memset(vbd[i][F * h:F * h + F, :, E + h:E + h + 1, :], 1.0)
        last.then_inc(S["vbd_ready"], 1)
        for i in range(2):
            dve.memset(xf[i][:], 0.0).then_inc(S["xw_ready"], 1)
        dve.memset(rden[:], 0.0).then_inc(S["z_ready"], 1)
        dve.wait_ge(S["z_ready"], 1)

        def maximum(n, k, a):
            dve.wait_ge(S[f"s_done{a}"], after(n, k))
            scores = bank[4 + a][:, :].rearrange("p (a b) -> p a b", b=F)
            dve.tensor_reduce(smax[:, a, :], scores, AX.X, ALU.max).then_inc(S["max_step"], 1)
            dve.wait_ge(S["max_step"], after(n, k, 2) - 1 + a)
            if n >= 1:
                dve.wait_ge(S[f"exp_done{a}"], after(n - 1, k))
            dve.tensor_tensor(s[:, a, :, :], scores,
                              smax[:, a, :].rearrange("p (a o) -> p a o", o=1).to_broadcast([P, PAIRS, F]),
                              ALU.subtract).then_inc(S[f"s_sub{a}"], 1)

        def logit(n, k):
            t = INFLIGHT * (n // BODY + k) + n % INFLIGHT
            dve.wait_ge(S["x_ready"], after(n, k))
            dve.wait_ge(S["z_ready"], t + 1)
            dve.tensor_tensor(xw[:], xf[n % 2][:], wf[:].rearrange("p (o f) -> p o f", o=1).to_broadcast([P, PAIRS, F]),
                              ALU.mult).then_inc(S["xw_ready"], 1)
            dve.wait_ge(S["xw_ready"], t + 3)
            cols = bass.ds(t * PAIRS, PAIRS) if k is not 0 else slice(t * PAIRS, (t + 1) * PAIRS)
            dve.tensor_reduce(z[:, cols], xw[:], AX.X, ALU.add).then_inc(S["z_ready"], 1)

        def stages(m, k):
            if live(m - 1):
                maximum(m - 1, k, 0)
            if live(m - 4):
                n = m - 4
                dve.wait_ge(S["rstd_ready"], after(n, k))
                if n >= 1:
                    dve.wait_ge(S["xt_done"], after(n - 1, k))
                dve.tensor_tensor(xn[:], cen[:], rstd[:].rearrange("p (a o) -> p a o", o=1).to_broadcast([P, 2 * PQ, E]),
                                  ALU.mult).then_inc(S["xn_ready"], 1)
            if live(m - 1):
                maximum(m - 1, k, 1)
            if live(m - 2):
                n = m - 2
                dve.wait_ge(S["pv_done"], after(n, k))
                if n >= 1:
                    dve.wait_ge(S["ot_done"], after(n - 1, k))
                for a in range(2):
                    last = dve.reciprocal(rden[:, PQ * a:PQ * a + PQ, :],
                                          bank[6 + a][:, 0:4 * VC].rearrange("p (a c) -> p a c", a=4)[:, :, E:VC])
                last.then_inc(S["rden_ready"], 1)
                dve.wait_ge(S["rden_ready"], after(n, k))
                for a in range(2):
                    last = dve.tensor_tensor(
                        on[:, PQ * a:PQ * a + PQ, :].rearrange("p a (h d) -> p a h d", h=H),
                        bank[6 + a][:, 0:4 * VC].rearrange("p (a c) -> p a c", a=4)[:, :, 0:E]
                        .rearrange("p a (h d) -> p a h d", h=H),
                        rden[:, PQ * a:PQ * a + PQ, :].rearrange("p a (h o) -> p a h o", o=1).to_broadcast([P, PQ, H, HD]),
                        ALU.mult)
                last.then_inc(S["on_ready"], 1)
            if live(m - 3):
                n = m - 3
                dve.wait_ge(S["o_done"], after(n, k))
                dve.wait_ge(S["r_ready"], after(n, k))
                dve.tensor_tensor(y[:].rearrange("p a e -> p (a e)"), bank[0][:, :],
                                  r[n % 4][:].rearrange("p a c -> p (a c)"), ALU.add).then_inc(S["y_sum_ready"], 1)
                dve.wait_ge(S["y_sum_ready"], after(n, k))
                dve.tensor_scalar(y[:], y[:], 0.0, None, ALU.max).then_inc(S["y_ready"], 1)
                dve.wait_ge(S["y_ready"], after(n, k))
                dve.tensor_reduce(ysum[:], y[:], AX.X, ALU.add).then_inc(S["ysum_ready"], 1)
                dve.wait_ge(S["ysum_ready"], after(n, k))
                dve.scalar_tensor_tensor(cen[:], ysum[:].rearrange("p (a o) -> p a o", o=1).to_broadcast([P, 2 * PQ, E]),
                                         -1.0 / E, y[:], ALU.mult, ALU.add).then_inc(S["cen_ready"], 1)
            if live(m - 5) and (m - 5) % BODY // INFLIGHT == L - 1:
                logit(m - 5, k)
            if live(m - 3):
                n = m - 3
                dve.wait_ge(S["sq_ready"], after(n, k))
                dve.tensor_reduce(sqs[:], sq[:], AX.X, ALU.add).then_inc(S["sqs_ready"], 1)
                dve.wait_ge(S["sqs_ready"], after(n, k))
                if n >= 1:
                    dve.wait_ge(S["rstd_ready"], after(n - 1, k))
                dve.tensor_scalar(var[:], sqs[:], 1.0 / E, EPS, ALU.mult, ALU.add).then_inc(S["var_ready"], 1)

        over_slots(dve, stages)
        logit(SLOTS - 1, 0)
        dve.wait_ge(S["att_done"], 1)
        dve.tensor_tensor(res[:], bank[2][:, 0:NJ], dnn[:], ALU.add).then_inc(S["res_step"], 1)
        for i in range(2):
            dve.wait_ge(S["res_step"], i + 1)
            dve.tensor_scalar(res[:], res[:], bfd[:, i:i + 1], None, ALU.add).then_inc(S["res_step"], 1)

    @block.tensor
    def _(pe):
        def stages(m, k):
            if live(m - 1):
                n = m - 1
                pe.wait_ge(S["q_ready"], after(n, k))
                pe.wait_ge(S["kh_ready"], after(n, k))
                for a in range(2):
                    if n >= 1:
                        pe.wait_ge(S[f"pt_ready{a}"], after(n - 1, k))
                    for i in range(8):
                        pair = 8 * a + i
                        last = pe.matmul(bank[4 + a][E * (i % 2):E * (i % 2) + E, P * (i // 2):P * (i // 2) + P],
                                         qg[n % 2][:, pair, :, :], kh[n % 2][:, pair, :, :], start=True, stop=True)
                    last.then_inc(S[f"s_done{a}"], 1)
            if live(m - 3):
                n = m - 3
                pe.wait_ge(S["on_ready"], after(n, k))
                if m - 1 < SLOTS:
                    pe.wait_ge(S["q_ready"], after(m - 1, k))
                else:
                    pe.wait_ge(S["y_sum_ready"], after(n - 1, k))
                for a in range(PQ):
                    last = pe.transpose(bank[0][:, P * a:P * a + P], on[:, 2 * a:2 * a + 2, :], ident[:])
                last.then_inc(S["ot_done"], 1)
            if live(m - 2):
                n = m - 2
                pe.wait_ge(S["pt_ready0"], after(n, k))
                pe.wait_ge(S["pt_ready1"], after(n, k))
                pe.wait_ge(v_loaded[n % 2], after2(n, k, 64))
                if n >= 1:
                    pe.wait_ge(S["on_ready"], after(n - 1, k))
                for a in range(PQ):
                    for p4 in range(4):
                        pair = 4 * a + p4
                        for g in range(2):
                            c = VC * (2 * (a % 2) + g)
                            i = 2 * pair + g
                            last = pe.matmul(bank[6 + a // 2][F * p4:F * p4 + F, c:c + VC],
                                             pt[n % 2][:, i // 16, F * (i % 16):F * (i % 16) + F],
                                             vbd[n % 2][:, p4, :, PQ * g + a], start=True, stop=True)
                last.then_inc(S["pv_done"], 1)
            if live(m - 4):
                n = m - 4
                pe.wait_ge(S["xn_ready"], after(n, k))
                if m - 1 < SLOTS:
                    pe.wait_ge(S["k_ready"], after(m - 1, k))
                elif n >= 1:
                    pe.wait_ge(S["x_ready"], after(n - 1, k))
                for a in range(PQ):
                    last = pe.transpose(bank[1][:, P * a:P * a + P], xn[:, 2 * a:2 * a + 2, :], ident[:])
                last.then_inc(S["xt_done"], 1)
            if live(m - 3):
                n = m - 3
                ln = n % BODY // INFLIGHT
                pe.wait_ge(S["ot_ready"], after(n, k))
                pe.matmul(bank[0][:, :], ones3[:], over_groups(bias3[:, ln, 1, :]), start=True, stop=False)
                for a in range(PQ):
                    last = pe.matmul(bank[0][:, P * a:P * a + P], ot[:, P * a:P * a + P], w[:, ln, OC:OC + P],
                                     start=False, stop=(a == PQ - 1))
                last.then_inc(S["o_done"], 1)
            if live(m):
                l = m % BODY // INFLIGHT
                xs = x[m % INFLIGHT]
                if l == 0:
                    pe.wait_ge(x_loaded[m % INFLIGHT], 16 * (m // BODY + 1 + k))
                if m >= 4:
                    pe.wait_ge(S["x_ready"], after(m - 4, k))
                elif m >= 1:
                    pe.wait_ge(S["k_ready"], after(m - 1, k))
                pe.matmul(bank[1][:, :], w[:, l, KCOL:KCOL + P], xs[:], start=True, stop=True).then_inc(S["k_done"], 1)
                if m >= 3:
                    pe.wait_ge(S["y_sum_ready"], after(m - 3, k))
                elif m >= 1:
                    pe.wait_ge(S["q_ready"], after(m - 1, k))
                pe.matmul(bank[0][:, :], w[:, l, QC:QC + P], xs[:], start=True, stop=True).then_inc(S["q_done"], 1)
            if live(m - 1):
                n = m - 1
                for a in range(2):
                    pe.wait_ge(S[f"exp_done{a}"], after(n, k))
                    for i in range(4):
                        last = pe.transpose(bank[4 + a][:, P * i:P * i + P], pr[:, a, P * i:P * i + P], ident[:])
                    last.then_inc(S[f"pt_turned{a}"], 1)
            if live(m):
                if m >= 1:
                    pe.wait_ge(S["v_ready"], after(m - 1, k))
                for a in range(PQ):
                    last = pe.matmul(bank[2][:, P * a:P * a + P], xs[:, P * a:P * a + P], w[:, l, VCOL:VCOL + P],
                                     start=True, stop=True)
                last.then_inc(S["v_done"], 1)
                if m >= 1:
                    pe.wait_ge(S["r_ready"], after(m - 1, k))
                pe.matmul(bank[3][:, :], ones3[:], over_groups(bias3[:, l, 0, :]), start=True, stop=False)
                for a in range(PQ):
                    last = pe.matmul(bank[3][:, P * a:P * a + P], xs[:, P * a:P * a + P], w[:, l, RC:RC + P],
                                     start=False, stop=(a == PQ - 1))
                last.then_inc(S["r_done"], 1)

        over_slots(pe, stages)
        pe.wait_ge(S["z_ready"], NT + 1)
        for d in range(NDG):
            last = pe.matmul(bank[2][:, 2 * d:2 * d + 2], z[:, P * d:P * d + P], gmask[:], start=True, stop=True)
        last.then_inc(S["att_done"], 1)


def kernel(**inputs):
    import numpy as np
    import concourse.bacc as bacc
    from concourse.bass_utils import run_bass_kernel_spmd as run

    def n(name):
        return np.asarray(inputs["L0_rec_" + name])

    arrays = {
        "Xi": np.ascontiguousarray(inputs["r_Xi"]),
        "Xv": n("Xv"), "tables": n("tables"),
        "WqkvT": np.ascontiguousarray(n("Wqkv").transpose(0, 2, 1)),
        "bqkv": n("bqkv"),
        "WoT": np.ascontiguousarray(n("Wo").transpose(0, 2, 1)),
        "bo": n("bo"),
        "WrT": np.ascontiguousarray(n("Wr").T),
        "br": n("br"), "gamma": n("gamma"), "beta": n("beta"),
        "Wf": n("Wf"), "bf": n("bf"), "W1": n("W1"), "b1": n("b1"),
        "W2": n("W2"), "b2": n("b2"), "Wd": n("Wd"), "bd": n("bd"),
        "ident": np.eye(P, dtype=np.float32),
    }
    nc = bacc.Bacc("TRN2", target_bir_lowering=False, num_devices=1)
    args = [nc.dram_tensor(f"in_{k}", a.shape, mybir.dt.from_np(a.dtype), kind="ExternalInput").ap()
            for k, a in arrays.items()]
    args.append(nc.dram_tensor("out_y", (B, 1), F32, kind="ExternalOutput").ap())
    build(nc, *args)
    r = run(nc, [{f"in_{k}": a for k, a in arrays.items()}], core_ids=[0])
    return r.results[0]["out_y"]
```

```python
from contextlib import ExitStack

import concourse.bass as bass
from concourse import mybir

F32 = mybir.dt.float32
F32R = mybir.dt.float32r
BF16 = mybir.dt.bfloat16
I32 = mybir.dt.int32
ALU = mybir.AluOpType
ACT = mybir.ActivationFunctionType
AX = mybir.AxisListType

B, F, V, E, H, L = 2048, 32, 6250, 64, 4, 3
HD = E // H
D1, D2 = 1024, 512
P = 128
NJ = B // P
NDG = NJ // 2
PAIRS = 16
TOK = PAIRS * F
NT = B // (2 * PAIRS)
PB = P // PAIRS
PQ = PAIRS // 4
SLOTS = NT * L
INFLIGHT = 8
BODY = INFLIGHT * L
LEAD = INFLIGHT
AHEAD = 3
XB = 4
TURNS = (SLOTS - LEAD) // BODY
KC = F * E // P
KC2 = D1 // P
EPS = 1e-5
SCALE = 1.0 / float(HD) ** 0.5
VC = E + H


def equals(value, number):
    return isinstance(value, int) and value == number


def build(nc, Xi, Xv, tables, WqkvT, bqkv, WoT, bo, WrT, br, gamma, beta, Wf, bf,
          W1, b1, W2, b2, Wd, bd, ident_in, out):
    xT_dram = nc.dram_tensor("xT_scratch", (NT, P, TOK), F32, kind="Internal").ap()
    v_dram = nc.dram_tensor("v_scratch", (2, P, TOK), F32, kind="Internal").ap()
    with ExitStack() as ctx:
        def sb(name, shape, dt=F32, to=ctx):
            return to.enter_context(nc.sbuf_tensor(name, shape, dt))

        def sem(name):
            return ctx.enter_context(nc.semaphore(name))

        bank = [ctx.enter_context(nc.psum_tensor(f"bank{i}", [P, 512], F32)) for i in range(8)]
        C = {
            "ident": sb("ident", [P, P]),
            "dnn": sb("dnn", [P, NJ]),
            "w": sb("w", [P, L, 5 * P]),
            "bq": sb("bq", [P, L]),
            "bk": sb("bk", [P, L]),
            "bqm": sb("bqm", [P, L, 2]),
            "gmask": sb("gmask", [P, 2]),
            "qmask": sb("qmask", [P, 2]),
            "hmask": sb("hmask", [P, H]),
            "gam": sb("gam", [P, 1]),
            "bet": sb("bet", [P, 1]),
            "wf": sb("wf", [P, F]),
            "bfd": sb("bfd", [P, 2]),
            "br_b": sb("br_b", [P, P]),
            "bo_b": sb("bo_b", [P, L, P]),
            "mhalf": sb("mhalf", [P, 2 * PQ]),
        }
        phase_one(nc, sb, sem, bank, C, xT_dram, Xi, Xv, tables, WqkvT, bqkv, WoT, bo, WrT, br,
                  gamma, beta, Wf, bf, W1, b1, W2, b2, Wd, bd, ident_in)
        phase_two(nc, ctx, sb, sem, bank, C, xT_dram, v_dram, out)


def phase_one(nc, sb, sem, bank, C, xT_dram, Xi, Xv, tables, WqkvT, bqkv, WoT, bo, WrT, br,
              gamma, beta, Wf, bf, W1, b1, W2, b2, Wd, bd, ident_in):
    ident, dnn, w, bo_b = (C[x] for x in ("ident", "dnn", "w", "bo_b"))
    with ExitStack() as ph:
        def s1(name, shape, dt=F32):
            return sb(name, shape, dt, ph)

        w1 = s1("w1", [P, KC, D1])
        w2 = s1("w2", [P, KC2, D2])
        wd_b = s1("wd_b", [P, D2])
        bias_m = s1("bias_m", [3, D1 + D2])
        bias_m3 = s1("bias_m3", [3, D1 + D2], BF16)
        ones3 = s1("ones3", [3, P], BF16)
        keep = s1("keep", [3, 2])
        bv = s1("bv", [P, L])
        bv_b = s1("bv_b", [P, L, P])
        xi = s1("xi", [P, NJ * F], I32)
        neg = s1("neg", [P, NJ * F], I32)
        base = s1("base", [P, F], I32)
        xv = s1("xv", [P, NJ * F])
        idx = [s1(f"idx{u}", [P, F], I32) for u in range(2)]
        emb = [s1(f"emb{u}", [P, F, E]) for u in range(2)]
        pairs = s1("pairs", [P, F, E, 2])
        xt = s1("xt", [P, P, F])
        et = [s1(f"et{g}", [P, KC, P]) for g in range(2)]
        turn = s1("turn", [1, 1])
        h1 = s1("h1", [P, D1])
        h1t = s1("h1t", [P, KC2, P])
        h2 = s1("h2", [P, D2])
        h2w = s1("h2w", [P, D2])
        logit = s1("logit", [P, 1])

        xi_loaded = sem("xi_loaded")
        setup_loaded = sem("setup_loaded")
        b_loaded = sem("b_loaded")
        W1_PARTS = 4
        w1_loaded = [sem(f"w1_loaded{i}") for i in range(W1_PARTS)]
        w2_loaded = sem("w2_loaded")
        consts_zeroed = sem("consts_zeroed")
        consts_loaded = sem("consts_loaded")
        base_ready = sem("base_ready")
        idx_all = sem("idx_all")
        idx_cur = sem("idx_cur")
        gather_turn = sem("gather_turn")
        gathered = [sem(f"gathered{u}") for u in range(2)]
        prep = sem("prep")
        mlp_bias = sem("mlp_bias")
        bv_ready = sem("bv_ready")
        bv_done = sem("bv_done")
        scaled = sem("scaled")
        et_turned = sem("et_turned")
        et_copied = sem("et_copied")
        xt_turned = sem("xt_turned")
        xt_copied = sem("xt_copied")
        xt_stored = sem("xt_stored")
        h1_done = sem("h1_done")
        h1_relu = sem("h1_relu")
        h1t_turned = sem("h1t_turned")
        h1t_copied = sem("h1t_copied")
        h2_done = sem("h2_done")
        h2_relu = sem("h2_relu")
        dnn_done = sem("dnn_done")
        dnn_stored = sem("dnn_stored")
        QC, KCOL, VCOL, RC, OC = (i * P for i in range(5))

        block = ph.enter_context(nc.Block())

        def over_steps(eng, step, first, stop):
            for j in range(first, 2):
                step(j, j % 2, j // 2)
            turns = (min(stop, NJ - 1) - 2) // 2
            with eng.Fori(0, turns) as k:
                for g in range(2):
                    step(2 * k + 2 + g, g, k + 1)
            for j in range(2 + 2 * turns, stop):
                step(j, j % 2, j // 2)

        @block.sync
        def _(sp):
            sp.dma_start(xi[:], Xi.rearrange("(p j) f -> p (j f)", j=NJ)).then_inc(xi_loaded, 16)
            sp.dma_start(ident[:], ident_in).then_inc(setup_loaded, 16)
            sp.dma_start(xv[:], Xv.rearrange("(p j) f o -> p (j f o)", j=NJ)).then_inc(setup_loaded, 16)
            sp.dma_start(bias_m[:, 0:D1], b1.partition_broadcast(3)).then_inc(b_loaded, 16)
            sp.dma_start(bias_m[:, D1:D1 + D2], b2.partition_broadcast(3)).then_inc(b_loaded, 16)
            for i in range(W1_PARTS):
                c = slice(i * KC // W1_PARTS, (i + 1) * KC // W1_PARTS)
                sp.dma_start(w1[:, c, :], W1.rearrange("(c p) n -> p c n", p=P)[:, c, :]).then_inc(w1_loaded[i], 16)
            sp.dma_start(w2[:], W2.rearrange("(c p) n -> p c n", p=P)).then_inc(w2_loaded, 16)
            sp.dma_start(wd_b[:], Wd.rearrange("n o -> (n o)").partition_broadcast(P)).then_inc(w2_loaded, 16)
            sp.wait_ge(consts_zeroed, 1)
            for l in range(L):
                for g in range(2):
                    rows = slice(E * g, E * g + E)
                    for col, part_w in ((QC, WqkvT[l, :, 0:E]), (KCOL, WqkvT[l, :, E:2 * E]),
                                        (VCOL, WqkvT[l, :, 2 * E:3 * E]), (RC, WrT), (OC, WoT[l])):
                        sp.dma_start(w[rows, l, col + E * g:col + E * g + E], part_w).then_inc(consts_loaded, 16)
                    with nc.allow_non_contiguous_dma(reason="64 bias values"):
                        for b, at in ((C["bq"], 0), (C["bk"], E), (bv, 2 * E)):
                            sp.dma_start(b[rows, l:l + 1], bqkv[l, at:at + E].rearrange("(e o) -> e o", o=1)
                                         ).then_inc(consts_loaded, 16)
                    sp.dma_start(bo_b[:, l, rows], bo[l].partition_broadcast(P)).then_inc(consts_loaded, 16)
            with nc.allow_non_contiguous_dma(reason="small constants"):
                for g in range(2):
                    rows = slice(E * g, E * g + E)
                    sp.dma_start(C["gam"][rows, :], gamma.rearrange("(e o) -> e o", o=1)).then_inc(consts_loaded, 16)
                    sp.dma_start(C["br_b"][:, rows], br.partition_broadcast(P)).then_inc(consts_loaded, 16)
                    sp.dma_start(C["bet"][rows, :], beta.rearrange("(e o) -> e o", o=1)).then_inc(consts_loaded, 16)
                    sp.dma_start(C["wf"][rows, :], Wf.rearrange("(f e) o -> e (f o)", e=E)).then_inc(consts_loaded, 16)
                sp.dma_start(C["bfd"][:, 0:1], bf.partition_broadcast(P)).then_inc(consts_loaded, 16)
                sp.dma_start(C["bfd"][:, 1:2], bd.partition_broadcast(P)).then_inc(consts_loaded, 16)
            with sp.Fori(0, NDG) as d:
                sp.wait_ge(xt_copied, 8 * d + 8)
                for g in range(2):
                    sp.dma_start(xT_dram[bass.ds(d * PB, PB), E * g:E * g + E].rearrange("t p c -> p t c"),
                                 xt[g:P:2, :, :].rearrange("p (t a) f -> p t (a f)", t=PB)).then_inc(xt_stored, 16)
            sp.wait_ge(xt_stored, 32 * NDG)

        n_consts = 16 * (L * 2 * 9 + 8 + 2)

        @block.gpsimd
        def _(pool):
            pool.iota(base[:], [[V, F]], base=0, channel_multiplier=0).then_inc(base_ready, 1)
            pool.memset(turn[:], 0.0).then_inc(base_ready, 1)
            pool.memset(C["mhalf"][:], -0.5).then_inc(base_ready, 1)
            pool.wait_ge(base_ready, 3)
            pool.wait_ge(idx_all, 4)
            rows = tables.rearrange("f v e -> (f v) e")

            def step(j, g, half):
                if not equals(half, 0):
                    pool.wait_ge(gathered[g], 16 * F * half)
                    pool.wait_ge(scaled, j - 1)
                pool.tensor_copy(idx[g][:], xi[:, bass.ds(j * F, F)] if not equals(half, 0)
                                 else xi[:, j * F:j * F + F]).then_inc(idx_cur, 1)
                pool.wait_ge(idx_cur, j + 1)
                pool.tensor_tensor(turn[:], turn[:], turn[:], ALU.mult).then_inc(gather_turn, 1)
                for f in range(F):
                    pool.indirect_dma_start(emb[g][:, f, :], None, rows,
                                            bass.IndirectOffsetOnAxis(idx[g][:, f:f + 1], 0)
                                            ).then_inc(gathered[g], 16)

            over_steps(pool, step, 0, NJ)

        @block.vector
        def _(dve):
            dve.memset(ones3[:], 1.0).then_inc(prep, 1)
            dve.memset(w[:], 0.0).then_inc(consts_zeroed, 1)
            dve.wait_ge(xi_loaded, 16)
            dve.tensor_scalar(neg[:], xi[:], 0.0, float(V), ALU.is_lt, ALU.mult).then_inc(idx_all, 1)
            dve.wait_ge(idx_all, 1)
            dve.tensor_tensor(neg[:], xi[:], neg[:], ALU.add).then_inc(idx_all, 1)
            dve.wait_ge(idx_all, 2)
            dve.tensor_scalar(neg[:], neg[:], float(V - 1), 0.0, ALU.min, ALU.max).then_inc(idx_all, 1)
            dve.wait_ge(idx_all, 3)
            dve.wait_ge(base_ready, 3)
            dve.tensor_tensor(xi[:].rearrange("p (j f) -> p j f", f=F), neg[:].rearrange("p (j f) -> p j f", f=F),
                              base[:].rearrange("p (o f) -> p o f", o=1).to_broadcast([P, NJ, F]),
                              ALU.add).then_inc(idx_all, 1)
            dve.wait_ge(setup_loaded, 32)
            dve.tensor_scalar(keep[:, 0:1], ident[0:3, 0:1], 1.0, None, ALU.subtract).then_inc(prep, 1)
            dve.tensor_scalar(keep[:, 1:2], ident[0:3, 2:3], -1.0, None, ALU.mult).then_inc(prep, 1)
            dve.wait_ge(prep, 3)
            dve.wait_ge(b_loaded, 32)

            for i in range(2):
                dve.tensor_copy(bias_m3[:], bias_m[:]).then_inc(mlp_bias, 1)
                dve.wait_ge(mlp_bias, 2 * i + 1)
                dve.scalar_tensor_tensor(bias_m[:], bias_m3[:], keep[:, i:i + 1], bias_m[:],
                                         ALU.mult, ALU.add).then_inc(mlp_bias, 1)
                dve.wait_ge(mlp_bias, 2 * i + 2)
            dve.tensor_copy(bias_m3[:], bias_m[:]).then_inc(mlp_bias, 1)

            def scale(j, g, half):
                dve.wait_ge(gathered[g], 16 * F * (half + 1))
                if not equals(half, 0):
                    dve.wait_ge(xt_turned, 8 * half)
                xvj = xv[:, bass.ds(j * F, F)] if not equals(half, 0) else xv[:, j * F:j * F + F]
                dve.tensor_tensor(pairs[:, :, :, g], emb[g][:],
                                  xvj.rearrange("p (f o) -> p f o", o=1).to_broadcast([P, F, E]),
                                  ALU.mult).then_inc(scaled, 1)

            def copy_et(j, g, c):
                dve.wait_ge(et_turned, 4 * j + c + 1)
                dve.tensor_copy(et[g][:, 4 * c:4 * c + 4, :],
                                bank[(2, 3, 7, 2)[c]][:, :].rearrange("p (a b) -> p a b", a=4)).then_inc(et_copied, 1)

            def copy_h1t(j, c):
                dve.wait_ge(h1t_turned, 2 * j + c + 1)
                dve.tensor_copy(h1t[:, 4 * c:4 * c + 4, :],
                                bank[(3, 7)[c]][:, :].rearrange("p (a b) -> p a b", a=4)).then_inc(h1t_copied, 1)

            def step(j, g, half):
                if not equals(j, 0):
                    for c in range(2):
                        copy_h1t(j - 1, c)
                if not equals(j, NJ - 1) and not equals(j, NJ):
                    scale(j + 1, 1 - g, half + g)
                    for c in range(4):
                        copy_et(j + 1, 1 - g, c)
                if not equals(j, 0):
                    dve.wait_ge(h2_relu, j)
                    dve.tensor_tensor_reduce(h2w[:], h2[:], wd_b[:], 1.0, 0.0, ALU.mult, ALU.add,
                                             logit[:]).then_inc(dnn_done, 1)
                    dve.wait_ge(dnn_done, j)
                    dve.tensor_copy(dnn[:, bass.ds(j - 1, 1)] if not isinstance(j, int) else dnn[:, j - 1:j],
                                    logit[:]).then_inc(dnn_stored, 1)
                    dve.wait_ge(dnn_stored, j)

            scale(0, 0, 0)
            for c in range(4):
                copy_et(0, 0, c)
            dve.wait_ge(w2_loaded, 32)
            over_steps(dve, step, 0, NJ + 1)

            gmask, hmask, qmask = C["gmask"], C["hmask"], C["qmask"]
            dve.wait_ge(consts_loaded, n_consts)
            dve.tensor_copy(bv_b[:], bv[:].rearrange("p (l o) -> p l o", o=1).to_broadcast([P, L, P])).then_inc(bv_ready, 1)
            dve.tensor_reduce(gmask[:], ident[:].rearrange("p (g c) -> p g c", g=2), AX.X, ALU.add).then_inc(prep, 1)
            dve.tensor_reduce(hmask[:], ident[:].rearrange("p (g h d) -> p h g d", g=2, h=H), AX.XY, ALU.add).then_inc(prep, 1)
            dve.wait_ge(prep, 5)
            dve.tensor_scalar(qmask[:], gmask[:], SCALE, None, ALU.mult).then_inc(prep, 1)
            dve.wait_ge(prep, 6)
            for g in range(2):
                dve.tensor_scalar(C["bqm"][:, :, g], C["bq"][:], qmask[:, g:g + 1], None, ALU.mult).then_inc(prep, 1)
            dve.wait_ge(bv_done, 1)
            dve.tensor_tensor(bo_b[:], bo_b[:],
                              bank[6][:, 0:L * P].rearrange("p (l c) -> p l c", l=L), ALU.add).then_inc(prep, 1)

        @block.scalar
        def _(act):
            def step(j, g, half):
                if not equals(j, NJ):
                    for n in range(2):
                        act.wait_ge(h1_done, 2 * j + n + 1)
                        act.activation(h1[:, 512 * n:512 * n + 512], bank[4 + n][:, :], ACT.Relu).then_inc(h1_relu, 1)
                    if g == 0:
                        if not equals(half, 0):
                            act.wait_ge(xt_stored, 32 * half)
                        for c in range(8):
                            act.wait_ge(xt_turned, 8 * half + c + 1)
                            act.activation(xt[:, :, 4 * c:4 * c + 4].rearrange("p a f -> p f a"),
                                           bank[c % 2][:, :].rearrange("p (f a) -> p f a", f=4),
                                           ACT.Copy).then_inc(xt_copied, 1)
                if not equals(j, 0):
                    act.wait_ge(h2_done, j)
                    if not equals(j, 1):
                        act.wait_ge(dnn_done, j - 1)
                    act.activation(h2[:], bank[6][:, :], ACT.Relu).then_inc(h2_relu, 1)

            over_steps(act, step, 0, NJ + 1)

        @block.tensor
        def _(pe):
            def turn_et(j, g, c):
                for i in range(4):
                    f = 2 * (4 * c + i)
                    last = pe.transpose(bank[(2, 3, 7, 2)[c]][:, P * i:P * i + P],
                                        pairs[:, f:f + 2, :, g].rearrange("p f e -> p (f e)"), ident[:])
                last.then_inc(et_turned, 1)

            def turn_h1(c):
                for i in range(4):
                    m = 4 * c + i
                    last = pe.transpose(bank[(3, 7)[c]][:, P * i:P * i + P], h1[:, P * m:P * m + P], ident[:])
                last.then_inc(h1t_turned, 1)

            def half_h1(j, g, n):
                if not equals(j, 0):
                    pe.wait_ge(h1_relu, 2 * (j - 1) + n + 1)
                cols = slice(512 * n, 512 * n + 512)
                pe.matmul(bank[4 + n][:, :], ones3[:], bias_m3[:, cols], start=True, stop=False)
                for c in range(KC):
                    if equals(j, 0) and n == 0 and c % (KC // W1_PARTS) == 0:
                        pe.wait_ge(w1_loaded[c * W1_PARTS // KC], 16)
                    last = pe.matmul(bank[4 + n][:, :], et[g][:, c, :], w1[:, c, cols],
                                     start=False, stop=(c == KC - 1))
                last.then_inc(h1_done, 1)

            def step(j, g, half):
                if not equals(j, NJ):
                    pe.wait_ge(et_copied, 4 * j + 4)
                if not equals(j, 0):
                    pe.wait_ge(h1_relu, 2 * j)
                    for c in range(2):
                        turn_h1(c)
                if not equals(j, NJ):
                    for n in range(2):
                        half_h1(j, g, n)
                if not equals(j, NJ - 1) and not equals(j, NJ):
                    pe.wait_ge(scaled, j + 2)
                    if not equals(j, 0):
                        pe.wait_ge(h1t_copied, 2 * j)
                    for c in range(4):
                        if c == 3:
                            pe.wait_ge(et_copied, 4 * (j + 1) + 1)
                        turn_et(j + 1, 1 - g, c)
                if g == 0 and not equals(j, NJ):
                    for c in range(8):
                        if not equals(half, 0) or c >= 2:
                            pe.wait_ge(xt_copied, 8 * half + c - 1)
                        for i in range(4):
                            last = pe.transpose(bank[c % 2][:, P * i:P * i + P],
                                                pairs[:, 4 * c + i, :, :].rearrange("p e g -> p (e g)"), ident[:])
                        last.then_inc(xt_turned, 1)
                if not equals(j, 0):
                    if not equals(j, 1):
                        pe.wait_ge(h2_relu, j - 1)
                    else:
                        pe.wait_ge(w2_loaded, 32)
                    pe.matmul(bank[6][:, :], ones3[:], bias_m3[:, D1:D1 + D2], start=True, stop=False)
                    pe.wait_ge(h1t_copied, 2 * j)
                    for c in range(KC2):
                        last = pe.matmul(bank[6][:, :], h1t[:, c, :], w2[:, c, :],
                                         start=False, stop=(c == KC2 - 1))
                    last.then_inc(h2_done, 1)

            pe.wait_ge(setup_loaded, 32)
            pe.wait_ge(scaled, 1)
            for c in range(4):
                if c == 3:
                    pe.wait_ge(et_copied, 1)
                turn_et(0, 0, c)
            pe.wait_ge(mlp_bias, 5)
            over_steps(pe, step, 0, NJ + 1)
            pe.wait_ge(bv_ready, 1)
            pe.wait_ge(h2_relu, NJ)
            for l in range(L):
                last = pe.matmul(bank[6][:, P * l:P * l + P], bv_b[:, l, :], w[:, l, OC:OC + P], start=True, stop=True)
            last.then_inc(bv_done, 1)


def phase_two(nc, ctx, sb, sem, bank, C, xT_dram, v_dram, out):
    QC, KCOL, VCOL, RC, OC = (i * P for i in range(5))
    ident, dnn, w, bk, bqm, gmask, qmask, hmask, gam, bet, wf, bfd, br_b, bo_b, mhalf = (
        C[n] for n in "ident dnn w bk bqm gmask qmask hmask gam bet wf bfd br_b bo_b mhalf".split())
    turn = sb("turn2", [1, 1])

    wh = sb("wh", [P, L, 4 * P], F32R)
    wl = sb("wl", [P, L, 4 * P], F32R)

    x = [sb(f"x{i}", [P, TOK]) for i in range(XB)]
    xh = [sb(f"xh{i}", [P, TOK], F32R) for i in range(XB)]
    xl = [sb(f"xl{i}", [P, TOK], F32R) for i in range(XB)]
    xf = [sb(f"xf{i}", [P, PAIRS, F]) for i in range(2)]
    xw = sb("xw", [P, PAIRS, F])
    z = sb("z", [P, NT * PAIRS])
    kt = sb("kt", [P, TOK])
    qg = [sb(f"qg{i}", [P, PAIRS, 2, F]) for i in range(2)]
    kh = [sb(f"kh{i}", [P, PAIRS, H, F]) for i in range(2)]
    v = [sb(f"v{i}", [P, E, 2, PQ]) for i in range(2)]
    vbd = [sb(f"vbd{i}", [P, 4, VC, 2 * PQ]) for i in range(3)]
    r = [sb(f"r{i}", [P, PQ, P]) for i in range(4)]
    smax = sb("smax", [P, 2, PAIRS])
    s = sb("s", [P, 2, PAIRS, F])
    pr = sb("pr", [P, 2, PAIRS * F])
    pt = [sb(f"pt{i}", [P, 2, PAIRS * F]) for i in range(2)]
    rden = sb("rden", [P, 2 * PQ, H])
    on = sb("on", [P, 2 * PQ, E])
    ot = sb("ot", [P, TOK])
    y = sb("y", [P, 2 * PQ, E])
    ysum = sb("ysum", [P, 2 * PQ])
    cen = sb("cen", [P, 2 * PQ, E])
    sq = sb("sq", [P, 2 * PQ, E])
    sqs = sb("sqs", [P, 2 * PQ])
    var = sb("var", [P, 2 * PQ])
    rstd = sb("rstd", [P, 2 * PQ])
    xn = sb("xn", [P, 2 * PQ, E])
    res = sb("res", [P, NJ])

    names = """turn_ready vbd_zeroed vbd_ready
        wh_ready wl_ready xh_ready xl_ready
        k_done q_done vr_done s_done0 s_done1 pv_done ot_done o_done xt_done r_sum r_max rb_ready
        k_ready q_ready kh_turn kh_ready r_ready v_ready ot_ready x_ready
        max_ready0 max_ready1 s_sub0 s_sub1 exp_done0 exp_done1 pt_turned0 pt_turned1 pt_ready0 pt_ready1
        rden_ready on_ready y_sum_ready y_ready ysum_ready cen_ready sq_ready sqs_ready var_ready
        rstd_ready xn_ready xw_ready z_ready att_done res_step out_stored""".split()
    S = {n: sem(n) for n in names}
    x_loaded = [sem(f"x_loaded{i}") for i in range(XB)]
    v_stored = [sem(f"v_stored{i}") for i in range(2)]
    v_loaded = [sem(f"v_loaded{i}") for i in range(3)]

    def after(b, k, per=1):
        return (b + 1) * per + BODY * per * k

    def after_of(b, k, per, n):
        return (b // n + 1) * per + BODY // n * per * k

    def loads_of_x(b, k):
        i = b % BODY // XB
        return (b // BODY * (INFLIGHT // XB) + i + 1) * 16 + INFLIGHT // XB * 16 * k

    def over_slots(eng, stages):
        for m in range(LEAD):
            stages(m, 0)
        with eng.Fori(0, TURNS) as k:
            for m in range(LEAD, LEAD + BODY):
                stages(m, k)
        for m in range(LEAD + BODY * TURNS, SLOTS + 6):
            stages(m, 0)

    def over_groups(row):
        return row.rearrange("p (o c) -> p o c", o=1).to_broadcast([P, PQ, P])

    def live(n):
        return 0 <= n < SLOTS

    block = ctx.enter_context(nc.Block())

    @block.sync
    def _(sp):
        def load_x(b, k):
            i = b % XB
            tile = INFLIGHT * (b // BODY) + b % BODY
            if not equals(k, 0) or b >= XB:
                sp.wait_ge(S["xl_ready"], after(b - XB, k))
            sp.dma_start(x[i][:], xT_dram[bass.ds(INFLIGHT * k + tile, 1)].rearrange("t p c -> (t p) c")
                         if not equals(k, 0) else xT_dram[tile]).then_inc(x_loaded[i], 16)

        def stages(m, k):
            n = m + AHEAD + 1
            if live(n) and n % BODY < INFLIGHT:
                load_x(n, k)
            if live(m - 1):
                n = m - 1
                i = n % 2
                if n < 3:
                    sp.wait_ge(S["vbd_ready"], 1)
                sp.wait_ge(S["v_ready"], after(n, k))
                sp.dma_start(v_dram[i], v[i][:, :, :, :].rearrange("p e g a -> p (e g a)")).then_inc(v_stored[i], 16)
                sp.wait_ge(v_stored[i], after_of(n, k, 16, 2))
                src = v_dram[i].rearrange("(a t) (h c) -> h t a c", a=4, h=H)
                for h in range(H):
                    sp.dma_start(vbd[n % 3][F * h:F * h + F, :, HD * h:HD * h + HD, :].rearrange("t a d c -> t a (d c)"),
                                 src[h]).then_inc(v_loaded[n % 3], 16)

        for b in range(AHEAD + 1):
            load_x(b, 0)
        over_slots(sp, stages)
        sp.wait_ge(S["res_step"], 3)
        sp.dma_start(out.rearrange("(p j) o -> p (j o)", j=NJ), res[:]).then_inc(S["out_stored"], 16)
        sp.wait_ge(S["out_stored"], 16)

    @block.gpsimd
    def _(pool):
        pool.memset(turn[:], 0.0).then_inc(S["turn_ready"], 1)
        pool.wait_ge(S["turn_ready"], 1)
        for i in range(3):
            pool.memset(vbd[i][:, :, :, :], 0.0).then_inc(S["vbd_zeroed"], 1)

        def stages(m, k):
            if live(m):
                i = m % 2
                pool.wait_ge(S["k_ready"], after(m, k))
                if m >= 2:
                    pool.wait_ge(S["s_done1"], after(m - 2, k))
                pool.tensor_tensor(turn[:], turn[:], turn[:], ALU.mult).then_inc(S["kh_turn"], 1)
                for h in range(H):
                    last = pool.tensor_scalar(kh[i][:, :, h, :], kt[:].rearrange("p (a f) -> p a f", f=F),
                                              hmask[:, h:h + 1], 1.0, ALU.mult, ALU.mult)
                last.then_inc(S["kh_ready"], 1)
            if live(m - 1):
                n = m - 1
                rows = r[n % 4]
                pool.wait_ge(S["r_max"], after(n, k))
                pool.tensor_tensor(rows[:], rows[:], over_groups(bo_b[:, n % BODY // INFLIGHT, :]),
                                   ALU.add).then_inc(S["rb_ready"], 1)
            if live(m - 4):
                pool.wait_ge(S["var_ready"], after(m - 4, k))
                pool.tensor_tensor(rstd[:], var[:], mhalf[:], ALU.pow).then_inc(S["rstd_ready"], 1)
            if live(m):
                rows = r[m % 4]
                pool.wait_ge(S["r_ready"], after(m, k))
                pool.tensor_tensor(rows[:], rows[:], over_groups(br_b[:]), ALU.add).then_inc(S["r_sum"], 1)

        over_slots(pool, stages)

    @block.scalar
    def _(act):
        def copy_x(c, k):
            if c < 0:
                return
            if live(c) and c % BODY < INFLIGHT:
                act.wait_ge(x_loaded[c % XB], loads_of_x(c, k))
                if c >= XB:
                    act.wait_ge(S["vr_done"], after(c - XB, k))
                act.activation(xh[c % XB][:], x[c % XB][:], ACT.Copy).then_inc(S["xh_ready"], 1)
            n = c - INFLIGHT
            if live(n):
                act.wait_ge(S["xt_done"], after(n, k))
                if n % BODY // INFLIGHT == L - 1:
                    act.wait_ge(S["xw_ready"], 1 + INFLIGHT * (n // BODY + k) + n % INFLIGHT)
                    dst = xf[n % 2][:, :, :].rearrange("p a f -> p (a f)")
                else:
                    act.activation(xh[c % XB][:], bank[1][:, :], ACT.Identity, bias=bet[:, 0:1],
                                   scale=gam[:, 0:1]).then_inc(S["xh_ready"], 1)
                    dst = x[c % XB][:]
                act.activation(dst, bank[1][:, :], ACT.Identity, bias=bet[:, 0:1], scale=gam[:, 0:1]).then_inc(S["x_ready"], 1)

        def stages(m, k):
            if live(m - 1):
                rows = r[(m - 1) % 4]
                act.wait_ge(S["r_sum"], after(m - 1, k))
                act.activation(rows[:], rows[:], ACT.Relu).then_inc(S["r_max"], 1)
            if live(m):
                l = m % BODY // INFLIGHT
                act.wait_ge(S["k_done"], after(m, k))
                if m >= 1:
                    act.wait_ge(S["kh_ready"], after(m - 1, k))
                act.activation(kt[:], bank[1][:, :], ACT.Identity, bias=bk[:, l:l + 1]).then_inc(S["k_ready"], 1)
            if live(m - 2):
                for a in range(2):
                    turned(m - 2, k, a)
            if live(m):
                act.wait_ge(S["q_done"], after(m, k))
                if m >= 2:
                    act.wait_ge(S["s_done1"], after(m - 2, k))
                for g in range(2):
                    last = query(m, g)
                last.then_inc(S["q_ready"], 1)
            if live(m - 4):
                act.wait_ge(S["cen_ready"], after(m - 4, k))
                if m >= 5:
                    act.wait_ge(S["sqs_ready"], after(m - 5, k))
                act.activation(sq[:, :, :], cen[:, :, :], ACT.Square).then_inc(S["sq_ready"], 1)
            copy_x(m + AHEAD, k)
            if live(m):
                act.wait_ge(S["vr_done"], after(m, k))
                if m >= 2:
                    act.wait_ge(v_stored[m % 2], after_of(m - 2, k, 16, 2))
                if m >= 3:
                    act.wait_ge(S["pv_done"], after(m - 3, k))
                for a in range(2):
                    last = act.activation(v[m % 2][:, :, :, 2 * a:2 * a + 2].rearrange("p e g a -> p a g e"),
                                          bank[2 + a][:, :].rearrange("p (a c) -> p a c", a=2)[:, :, 0:P]
                                          .rearrange("p a (g e) -> p a g e", g=2), ACT.Copy)
                last.then_inc(S["v_ready"], 1)
                if m >= 4:
                    act.wait_ge(S["y_sum_ready"], after(m - 4, k))
                for a in range(2):
                    last = act.activation(r[m % 4][:, 2 * a:2 * a + 2, :],
                                          bank[2 + a][:, :].rearrange("p (a c) -> p a c", a=2)[:, :, P:2 * P], ACT.Copy)
                last.then_inc(S["r_ready"], 1)
            if live(m - 3):
                act.wait_ge(S["ot_done"], after(m - 3, k))
                if m >= 4:
                    act.wait_ge(S["o_done"], after(m - 4, k))
                act.activation(ot[:], bank[0][:, :], ACT.Copy).then_inc(S["ot_ready"], 1)
            if live(m - 1):
                exp(m - 1, k, 0)
                exp(m - 1, k, 1)

        def query(m, g):
            l = m % BODY // INFLIGHT
            return act.activation(qg[m % 2][:, :, g, :], bank[0][:, :].rearrange("p (a f) -> p a f", f=F),
                                  ACT.Identity, bias=bqm[:, l, g:g + 1], scale=qmask[:, g:g + 1])

        def exp(n, k, a):
            act.wait_ge(S[f"s_sub{a}"], after(n, k))
            if n >= 1:
                act.wait_ge(S[f"pt_turned{a}"], after(n - 1, k))
            act.activation(pr[:, a, :], s[:, a, :, :].rearrange("p a b -> p (a b)"), ACT.Exp).then_inc(S[f"exp_done{a}"], 1)

        def turned(n, k, a):
            act.wait_ge(S[f"pt_turned{a}"], after(n, k))
            if n >= 2 and a == 0:
                act.wait_ge(S["pv_done"], after(n - 2, k))
            act.activation(pt[n % 2][:, a, :], bank[4 + a][:, :], ACT.Copy).then_inc(S[f"pt_ready{a}"], 1)

        for c in range(AHEAD):
            copy_x(c, 0)
        over_slots(act, stages)

    @block.vector
    def _(dve):
        def split_weights(l):
            dve.tensor_copy(wh[:, l, :], w[:, l, 0:4 * P]).then_inc(S["wh_ready"], 1)
            dve.wait_ge(S["wh_ready"], l + 1)
            dve.tensor_tensor(wl[:, l, :], w[:, l, 0:4 * P], wh[:, l, :], ALU.subtract).then_inc(S["wl_ready"], 1)

        split_weights(0)
        for i in range(2):
            dve.memset(xf[i][:], 0.0).then_inc(S["xw_ready"], 1)
        dve.memset(rden[:], 0.0).then_inc(S["z_ready"], 1)
        dve.wait_ge(S["z_ready"], 1)

        def scores(a):
            return bank[4 + a][:, :].rearrange("p (a b) -> p a b", b=F)

        def maximum(n, k, a):
            dve.wait_ge(S[f"s_done{a}"], after(n, k))
            if n >= 1:
                dve.wait_ge(S[f"s_sub{a}"], after(n - 1, k))
            dve.tensor_reduce(smax[:, a, :], scores(a), AX.X, ALU.max).then_inc(S[f"max_ready{a}"], 1)

        def subtract(n, k, a):
            dve.wait_ge(S[f"max_ready{a}"], after(n, k))
            if n >= 1:
                dve.wait_ge(S[f"exp_done{a}"], after(n - 1, k))
            dve.tensor_tensor(s[:, a, :, :], scores(a),
                              smax[:, a, :].rearrange("p (a o) -> p a o", o=1).to_broadcast([P, PAIRS, F]),
                              ALU.subtract).then_inc(S[f"s_sub{a}"], 1)

        def logit(n, k):
            t = INFLIGHT * (n // BODY + k) + n % INFLIGHT
            dve.wait_ge(S["x_ready"], after(n, k))
            dve.wait_ge(S["z_ready"], t + 1)
            dve.tensor_tensor(xw[:], xf[n % 2][:], wf[:].rearrange("p (o f) -> p o f", o=1).to_broadcast([P, PAIRS, F]),
                              ALU.mult).then_inc(S["xw_ready"], 1)
            dve.wait_ge(S["xw_ready"], t + 3)
            cols = bass.ds(t * PAIRS, PAIRS) if not equals(k, 0) else slice(t * PAIRS, (t + 1) * PAIRS)
            dve.tensor_reduce(z[:, cols], xw[:], AX.X, ALU.add).then_inc(S["z_ready"], 1)

        def lower_x(c, k):
            if live(c):
                dve.wait_ge(S["xh_ready"], after(c, k))
                if c % BODY >= INFLIGHT:
                    dve.wait_ge(S["x_ready"], after(c - INFLIGHT, k))
                if c >= XB:
                    dve.wait_ge(S["vr_done"], after(c - XB, k))
                dve.tensor_tensor(xl[c % XB][:], x[c % XB][:], xh[c % XB][:], ALU.subtract).then_inc(S["xl_ready"], 1)

        def stages(m, k):
            if live(m - 4):
                n = m - 4
                dve.wait_ge(S["o_done"], after(n, k))
                dve.wait_ge(S["rb_ready"], after(n, k))
                dve.tensor_tensor(y[:].rearrange("p a e -> p (a e)"), bank[0][:, :],
                                  r[n % 4][:].rearrange("p a c -> p (a c)"), ALU.add).then_inc(S["y_sum_ready"], 1)
                dve.wait_ge(S["y_sum_ready"], after(n, k))
                dve.tensor_scalar(y[:], y[:], 0.0, None, ALU.max).then_inc(S["y_ready"], 1)
                dve.wait_ge(S["y_ready"], after(n, k))
                dve.tensor_reduce(ysum[:], y[:], AX.X, ALU.add).then_inc(S["ysum_ready"], 1)
                dve.wait_ge(S["ysum_ready"], after(n, k))
                dve.scalar_tensor_tensor(cen[:], ysum[:].rearrange("p (a o) -> p a o", o=1).to_broadcast([P, 2 * PQ, E]),
                                         -1.0 / E, y[:], ALU.mult, ALU.add).then_inc(S["cen_ready"], 1)
            lower_x(m + AHEAD - 1, k)
            if live(m - 6) and (m - 6) % BODY // INFLIGHT == L - 1:
                logit(m - 6, k)
            if live(m - 4):
                n = m - 4
                dve.wait_ge(S["sq_ready"], after(n, k))
                dve.tensor_reduce(sqs[:], sq[:], AX.X, ALU.add).then_inc(S["sqs_ready"], 1)
                dve.wait_ge(S["sqs_ready"], after(n, k))
                if n >= 1:
                    dve.wait_ge(S["rstd_ready"], after(n - 1, k))
                dve.tensor_scalar(var[:], sqs[:], 1.0 / E, EPS, ALU.mult, ALU.add).then_inc(S["var_ready"], 1)
            if live(m - 1):
                for a in range(2):
                    maximum(m - 1, k, a)
                    subtract(m - 1, k, a)
            if live(m - 4):
                n = m - 4
                dve.wait_ge(S["rstd_ready"], after(n, k))
                if n >= 1:
                    dve.wait_ge(S["xt_done"], after(n - 1, k))
                dve.tensor_tensor(xn[:], cen[:], rstd[:].rearrange("p (a o) -> p a o", o=1).to_broadcast([P, 2 * PQ, E]),
                                  ALU.mult).then_inc(S["xn_ready"], 1)
            if live(m - 2):
                n = m - 2
                dve.wait_ge(S["pv_done"], after(n, k))
                if n >= 1:
                    dve.wait_ge(S["ot_done"], after(n - 1, k))
                for a in range(2):
                    last = dve.reciprocal(rden[:, PQ * a:PQ * a + PQ, :],
                                          bank[6 + a][:, 0:4 * VC].rearrange("p (a c) -> p a c", a=4)[:, :, E:VC])
                last.then_inc(S["rden_ready"], 1)
                dve.wait_ge(S["rden_ready"], after(n, k))
                for a in range(2):
                    last = dve.tensor_tensor(
                        on[:, PQ * a:PQ * a + PQ, :].rearrange("p a (h d) -> p a h d", h=H),
                        bank[6 + a][:, 0:4 * VC].rearrange("p (a c) -> p a c", a=4)[:, :, 0:E]
                        .rearrange("p a (h d) -> p a h d", h=H),
                        rden[:, PQ * a:PQ * a + PQ, :].rearrange("p a (h o) -> p a h o", o=1).to_broadcast([P, PQ, H, HD]),
                        ALU.mult)
                last.then_inc(S["on_ready"], 1)

        for c in range(AHEAD - 1):
            lower_x(c, 0)
        dve.wait_ge(S["vbd_zeroed"], 3)
        for i in range(3):
            for h in range(H):
                last = dve.memset(vbd[i][F * h:F * h + F, :, E + h:E + h + 1, :], 1.0)
        last.then_inc(S["vbd_ready"], 1)
        for l in range(1, L):
            split_weights(l)
        over_slots(dve, stages)
        dve.wait_ge(S["att_done"], 1)
        dve.tensor_tensor(res[:], bank[2][:, 0:NJ], dnn[:], ALU.add).then_inc(S["res_step"], 1)
        for i in range(2):
            dve.wait_ge(S["res_step"], i + 1)
            dve.tensor_scalar(res[:], res[:], bfd[:, i:i + 1], None, ALU.add).then_inc(S["res_step"], 1)

    @block.tensor
    def _(pe):
        def projection(out, col, l, i):
            pe.matmul(out, wh[:, l, col:col + P], xh[i][:], start=True, stop=False)
            pe.matmul(out, wl[:, l, col:col + P], xh[i][:], start=False, stop=False)
            return pe.matmul(out, wh[:, l, col:col + P], xl[i][:], start=False, stop=True)

        def stages(m, k):
            if live(m):
                l = m % BODY // INFLIGHT
                i = m % XB
                if m < LEAD:
                    pe.wait_ge(S["wl_ready"], 1 if m < LEAD - 1 else L)
                pe.wait_ge(S["xh_ready"], after(m, k))
                pe.wait_ge(S["xl_ready"], after(m, k))
                if m >= 6:
                    pe.wait_ge(S["x_ready"], after(m - 6, k))
                elif m >= 1:
                    pe.wait_ge(S["k_ready"], after(m - 1, k))
                projection(bank[1][:, :], KCOL, l, i).then_inc(S["k_done"], 1)
            if live(m - 2):
                n = m - 2
                for a in range(2):
                    pe.wait_ge(S[f"exp_done{a}"], after(n, k))
                    for c in range(4):
                        last = pe.transpose(bank[4 + a][:, P * c:P * c + P], pr[:, a, P * c:P * c + P], ident[:])
                    last.then_inc(S[f"pt_turned{a}"], 1)
            if live(m):
                if m >= 4:
                    pe.wait_ge(S["y_sum_ready"], after(m - 4, k))
                elif m >= 1:
                    pe.wait_ge(S["q_ready"], after(m - 1, k))
                projection(bank[0][:, :], QC, l, i).then_inc(S["q_done"], 1)
            if live(m - 5):
                n = m - 5
                pe.wait_ge(S["xn_ready"], after(n, k))
                if live(m):
                    pe.wait_ge(S["k_ready"], after(m, k))
                elif n >= 1:
                    pe.wait_ge(S["x_ready"], after(n - 1, k))
                for a in range(PQ):
                    last = pe.transpose(bank[1][:, P * a:P * a + P], xn[:, 2 * a:2 * a + 2, :], ident[:])
                last.then_inc(S["xt_done"], 1)
            if live(m):
                if m >= 1:
                    pe.wait_ge(S["r_ready"], after(m - 1, k))
                for half in range(2):
                    out = bank[2 + half]
                    for a in range(2):
                        cols = slice(256 * a, 256 * a + 256)
                        toks = slice(P * (2 * half + a), P * (2 * half + a) + P)
                        pe.matmul(out[:, cols], xh[i][:, toks], wh[:, l, VCOL:VCOL + 2 * P], start=True, stop=False)
                        pe.matmul(out[:, cols], xh[i][:, toks], wl[:, l, VCOL:VCOL + 2 * P], start=False, stop=False)
                        last = pe.matmul(out[:, cols], xl[i][:, toks], wh[:, l, VCOL:VCOL + 2 * P],
                                         start=False, stop=True)
                last.then_inc(S["vr_done"], 1)
            if live(m - 1):
                n = m - 1
                pe.wait_ge(S["q_ready"], after(n, k))
                pe.wait_ge(S["kh_ready"], after(n, k))
                for a in range(2):
                    if n >= 1:
                        pe.wait_ge(S[f"pt_ready{a}"], after(n - 1, k))
                    for i in range(8):
                        pair = 8 * a + i
                        last = pe.matmul(bank[4 + a][E * (i % 2):E * (i % 2) + E, P * (i // 2):P * (i // 2) + P],
                                         qg[n % 2][:, pair, :, :], kh[n % 2][:, pair, :, :], start=True, stop=True)
                    last.then_inc(S[f"s_done{a}"], 1)
            if live(m - 3):
                n = m - 3
                pe.wait_ge(S["on_ready"], after(n, k))
                if live(m):
                    pe.wait_ge(S["q_ready"], after(m, k))
                else:
                    pe.wait_ge(S["y_sum_ready"], after(n - 1, k))
                for a in range(PQ):
                    last = pe.transpose(bank[0][:, P * a:P * a + P], on[:, 2 * a:2 * a + 2, :], ident[:])
                last.then_inc(S["ot_done"], 1)
            if live(m - 2):
                n = m - 2
                pe.wait_ge(S["pt_ready0"], after(n, k))
                pe.wait_ge(S["pt_ready1"], after(n, k))
                pe.wait_ge(v_loaded[n % 3], after_of(n, k, 64, 3))
                if n >= 1:
                    pe.wait_ge(S["on_ready"], after(n - 1, k))
                for a in range(PQ):
                    for p4 in range(4):
                        pair = 4 * a + p4
                        for g in range(2):
                            c = VC * (2 * (a % 2) + g)
                            i = 2 * pair + g
                            last = pe.matmul(bank[6 + a // 2][F * p4:F * p4 + F, c:c + VC],
                                             pt[n % 2][:, i // 16, F * (i % 16):F * (i % 16) + F],
                                             vbd[n % 3][:, p4, :, PQ * g + a], start=True, stop=True)
                last.then_inc(S["pv_done"], 1)
            if live(m - 3):
                n = m - 3
                ln = n % BODY // INFLIGHT
                pe.wait_ge(S["ot_ready"], after(n, k))
                for a in range(PQ):
                    last = pe.matmul(bank[0][:, P * a:P * a + P], ot[:, P * a:P * a + P], w[:, ln, OC:OC + P],
                                     start=True, stop=True)
                last.then_inc(S["o_done"], 1)

        over_slots(pe, stages)
        pe.wait_ge(S["z_ready"], NT + 1)
        for d in range(NDG):
            last = pe.matmul(bank[2][:, 2 * d:2 * d + 2], z[:, P * d:P * d + P], gmask[:], start=True, stop=True)
        last.then_inc(S["att_done"], 1)


def kernel(**inputs):
    import numpy as np
    import concourse.bacc as bacc
    from concourse.bass_utils import run_bass_kernel_spmd as run

    def n(name):
        return np.asarray(inputs["L0_rec_" + name])

    arrays = {
        "Xi": np.ascontiguousarray(inputs["r_Xi"]),
        "Xv": n("Xv"), "tables": n("tables"),
        "WqkvT": np.ascontiguousarray(n("Wqkv").transpose(0, 2, 1)),
        "bqkv": n("bqkv"),
        "WoT": np.ascontiguousarray(n("Wo").transpose(0, 2, 1)),
        "bo": n("bo"),
        "WrT": np.ascontiguousarray(n("Wr").T),
        "br": n("br"), "gamma": n("gamma"), "beta": n("beta"),
        "Wf": n("Wf"), "bf": n("bf"), "W1": n("W1"), "b1": n("b1"),
        "W2": n("W2"), "b2": n("b2"), "Wd": n("Wd"), "bd": n("bd"),
        "ident": np.eye(P, dtype=np.float32),
    }
    nc = bacc.Bacc("TRN2", target_bir_lowering=False, num_devices=1)
    args = [nc.dram_tensor(f"in_{k}", a.shape, mybir.dt.from_np(a.dtype), kind="ExternalInput").ap()
            for k, a in arrays.items()]
    args.append(nc.dram_tensor("out_y", (B, 1), F32, kind="ExternalOutput").ap())
    build(nc, *args)
    r = run(nc, [{f"in_{k}": a for k, a in arrays.items()}], core_ids=[0])
    return r.results[0]["out_y"]
```
